# Optimizing a Trainium2 kernel written in Bass

```python
import numpy as np
import jax
import jax.numpy as jnp

def _softmax(x, axis=-1):
    return jax.nn.softmax(x, axis=axis)

def _gelu(x):
    return jax.nn.gelu(x, approximate=True)

def _silu(x):
    return jax.nn.silu(x)

def _sigmoid(x):
    return jax.nn.sigmoid(x)

def _layernorm(x, axis=-1, eps=1e-05):
    m = jnp.mean(x, axis=axis, keepdims=True)
    v = jnp.var(x, axis=axis, keepdims=True)
    return (x - m) / jnp.sqrt(v + eps)

def _scatter_add(tgt, idx, src, axis=0):
    return tgt.at[idx].add(src)

def _segment_sum(src, seg, n):
    return jax.ops.segment_sum(src, seg, n)
kernel_name = 'mk_conv_seq_d2_conv_nhwc256_r4_bc0e19'

def setup_inputs(seed: int=0):
    np.random.seed(seed)
    _w = jnp.asarray

    def _rec_inputs():
        import jax
        import jax.numpy as jnp
        _gk = jax.random.key(seed)
        x = -8.268e-05 + 0.9999 * jax.random.normal(jax.random.fold_in(_gk, 1), (16, 56, 56, 64), jnp.float32)
        return x
    x = _rec_inputs()

    def _L0_conv_setup():
        import jax, jax.numpy as jnp
        import numpy as np
        from jax.scipy.linalg import cholesky, solve_triangular
        EPS = 0.001
        key = jax.random.key(seed)
        k1, = jax.random.split(key, 1)
        b, w, h, c = (16, 56, 56, 64)
        x = jax.random.normal(k1, (b, w, h, c), dtype=jnp.float32)
        gamma = jnp.ones((c,), dtype=jnp.float32)
        beta = jnp.zeros((c,), dtype=jnp.float32)
        return {'x': x, 'gamma': gamma, 'beta': beta}
    _L0_conv_all = _L0_conv_setup()
    _L0_conv_in = {k: v for k, v in _L0_conv_all.items() if k in ('gamma', 'beta')}
    del _L0_conv_all

    def _L1_conv_setup():
        import jax, jax.numpy as jnp
        import numpy as np
        EPS = 1e-05
        LAM = 0.01
        NUM_BLOCKS = 8

        def layer_norm(x, g, b):
            mu = jnp.mean(x, axis=-1, keepdims=True)
            var = jnp.mean(jnp.square(x - mu), axis=-1, keepdims=True)
            return (x - mu) * jax.lax.rsqrt(var + EPS) * g + b

        def softshrink(v, lam):
            return jnp.where(jnp.abs(v) > lam, v - jnp.sign(v) * lam, jnp.zeros_like(v))

        def afno_filter(x, w1, b1, w2, b2):
            B, H, W, C = x.shape
            bs = C // NUM_BLOCKS
            xf = jnp.fft.rfft2(x, axes=(1, 2), norm='ortho')
            xf = xf.reshape(B, H, W // 2 + 1, NUM_BLOCKS, bs)
            xr, xi = (jnp.real(xf), jnp.imag(xf))
            o1r = jax.nn.relu(jnp.einsum('bhwni,nio->bhwno', xr, w1[0]) - jnp.einsum('bhwni,nio->bhwno', xi, w1[1]) + b1[0])
            o1i = jax.nn.relu(jnp.einsum('bhwni,nio->bhwno', xi, w1[0]) + jnp.einsum('bhwni,nio->bhwno', xr, w1[1]) + b1[1])
            o2r = jnp.einsum('bhwni,nio->bhwno', o1r, w2[0]) - jnp.einsum('bhwni,nio->bhwno', o1i, w2[1]) + b2[0]
            o2i = jnp.einsum('bhwni,nio->bhwno', o1i, w2[0]) + jnp.einsum('bhwni,nio->bhwno', o1r, w2[1]) + b2[1]
            o2r = softshrink(o2r, LAM)
            o2i = softshrink(o2i, LAM)
            yf = (o2r + 1j * o2i).reshape(B, H, W // 2 + 1, C)
            y = jnp.fft.irfft2(yf, s=(H, W), axes=(1, 2), norm='ortho')
            return y + x
        key = jax.random.key(seed)
        ks = jax.random.split(key, 16)
        B, H, W, C = (2, 64, 64, 64)
        bs = C // NUM_BLOCKS
        latent = 4 * C
        scale = 0.02
        return {'x': jax.random.normal(ks[0], (B, H, W, C), dtype=jnp.float32), 'n1_g': jnp.ones((C,), jnp.float32), 'n1_b': jnp.zeros((C,), jnp.float32), 'n2_g': jnp.ones((C,), jnp.float32), 'n2_b': jnp.zeros((C,), jnp.float32), 'w1': scale * jax.random.normal(ks[1], (2, NUM_BLOCKS, bs, bs), jnp.float32), 'b1': scale * jax.random.normal(ks[2], (2, NUM_BLOCKS, bs), jnp.float32), 'w2': scale * jax.random.normal(ks[3], (2, NUM_BLOCKS, bs, bs), jnp.float32), 'b2': scale * jax.random.normal(ks[4], (2, NUM_BLOCKS, bs), jnp.float32), 'mw1': jax.random.normal(ks[5], (C, latent), jnp.float32) / np.sqrt(C), 'mb1': jnp.zeros((latent,), jnp.float32), 'mw2': jax.random.normal(ks[6], (latent, C), jnp.float32) / np.sqrt(latent), 'mb2': jnp.zeros((C,), jnp.float32)}
    _L1_conv_all = _L1_conv_setup()
    _L1_conv_in = {k: v for k, v in _L1_conv_all.items() if k in ('n1_g', 'n1_b', 'n2_g', 'n2_b', 'w1', 'b1', 'w2', 'b2', 'mw1', 'mb1', 'mw2', 'mb2')}
    del _L1_conv_all
    return {'x': x, 'L0_conv_gamma': _L0_conv_in['gamma'], 'L0_conv_beta': _L0_conv_in['beta'], 'L1_conv_n1_g': _L1_conv_in['n1_g'], 'L1_conv_n1_b': _L1_conv_in['n1_b'], 'L1_conv_n2_g': _L1_conv_in['n2_g'], 'L1_conv_n2_b': _L1_conv_in['n2_b'], 'L1_conv_w1': _L1_conv_in['w1'], 'L1_conv_b1': _L1_conv_in['b1'], 'L1_conv_w2': _L1_conv_in['w2'], 'L1_conv_b2': _L1_conv_in['b2'], 'L1_conv_mw1': _L1_conv_in['mw1'], 'L1_conv_mb1': _L1_conv_in['mb1'], 'L1_conv_mw2': _L1_conv_in['mw2'], 'L1_conv_mb2': _L1_conv_in['mb2']}

def reference(x, L0_conv_gamma, L0_conv_beta, L1_conv_n1_g, L1_conv_n1_b, L1_conv_n2_g, L1_conv_n2_b, L1_conv_w1, L1_conv_b1, L1_conv_w2, L1_conv_b2, L1_conv_mw1, L1_conv_mb1, L1_conv_mw2, L1_conv_mb2):
    import jax
    import jax.numpy as jnp

    def _L0_conv_ref(x, gamma, beta):
        import jax, jax.numpy as jnp
        import numpy as np
        from jax.scipy.linalg import cholesky, solve_triangular
        EPS = 0.001
        b, w, h, c = x.shape
        n = b * w * h
        x_flat = jnp.transpose(x, (3, 0, 1, 2)).reshape(c, n)
        m = jnp.mean(x_flat, axis=1, keepdims=True)
        f = x_flat - m
        ff = f @ f.T / (jnp.float32(n) - 1.0)
        ff = (1.0 - EPS) * ff + EPS * jnp.eye(c, dtype=x.dtype)
        L = cholesky(ff, lower=True)
        inv_sqrt = solve_triangular(L, jnp.eye(c, dtype=x.dtype), lower=True)
        f_hat = inv_sqrt @ f
        out = jnp.transpose(f_hat.reshape(c, b, w, h), (1, 2, 3, 0))
        out = out * gamma.reshape(1, 1, 1, c) + beta.reshape(1, 1, 1, c)
        return out

    def _L1_conv_ref(x, n1_g, n1_b, n2_g, n2_b, w1, b1, w2, b2, mw1, mb1, mw2, mb2):
        import jax, jax.numpy as jnp
        import numpy as np
        EPS = 1e-05
        LAM = 0.01
        NUM_BLOCKS = 8

        def layer_norm(x, g, b):
            mu = jnp.mean(x, axis=-1, keepdims=True)
            var = jnp.mean(jnp.square(x - mu), axis=-1, keepdims=True)
            return (x - mu) * jax.lax.rsqrt(var + EPS) * g + b

        def softshrink(v, lam):
            return jnp.where(jnp.abs(v) > lam, v - jnp.sign(v) * lam, jnp.zeros_like(v))

        def afno_filter(x, w1, b1, w2, b2):
            B, H, W, C = x.shape
            bs = C // NUM_BLOCKS
            xf = jnp.fft.rfft2(x, axes=(1, 2), norm='ortho')
            xf = xf.reshape(B, H, W // 2 + 1, NUM_BLOCKS, bs)
            xr, xi = (jnp.real(xf), jnp.imag(xf))
            o1r = jax.nn.relu(jnp.einsum('bhwni,nio->bhwno', xr, w1[0]) - jnp.einsum('bhwni,nio->bhwno', xi, w1[1]) + b1[0])
            o1i = jax.nn.relu(jnp.einsum('bhwni,nio->bhwno', xi, w1[0]) + jnp.einsum('bhwni,nio->bhwno', xr, w1[1]) + b1[1])
            o2r = jnp.einsum('bhwni,nio->bhwno', o1r, w2[0]) - jnp.einsum('bhwni,nio->bhwno', o1i, w2[1]) + b2[0]
            o2i = jnp.einsum('bhwni,nio->bhwno', o1i, w2[0]) + jnp.einsum('bhwni,nio->bhwno', o1r, w2[1]) + b2[1]
            o2r = softshrink(o2r, LAM)
            o2i = softshrink(o2i, LAM)
            yf = (o2r + 1j * o2i).reshape(B, H, W // 2 + 1, C)
            y = jnp.fft.irfft2(yf, s=(H, W), axes=(1, 2), norm='ortho')
            return y + x
        residual = x
        h = layer_norm(x, n1_g, n1_b)
        h = afno_filter(h, w1, b1, w2, b2)
        h = h + residual
        residual = h
        h = layer_norm(h, n2_g, n2_b)
        h = jax.nn.gelu(h @ mw1 + mb1, approximate=False)
        h = h @ mw2 + mb2
        return h + residual

    def _gn(v, G=32, eps=1e-05):
        B_, H_, W_, C_ = v.shape
        g = v.reshape(B_, H_, W_, G, C_ // G)
        m = jnp.mean(g, axis=(1, 2, 4), keepdims=True)
        s = jnp.var(g, axis=(1, 2, 4), keepdims=True)
        return ((g - m) / jnp.sqrt(s + eps)).reshape(v.shape)

    def _ln_c(v, eps=1e-06):
        m = jnp.mean(v, axis=-1, keepdims=True)
        s = jnp.var(v, axis=-1, keepdims=True)
        return (v - m) / jnp.sqrt(s + eps)

    def _ln_t(v, eps=1e-05):
        m = jnp.mean(v, axis=-1, keepdims=True)
        s = jnp.var(v, axis=-1, keepdims=True)
        return (v - m) / jnp.sqrt(s + eps)

    def _to_tokens(v):
        B_, H_, W_, C_ = v.shape
        return v.reshape(B_, H_ * W_, C_)

    def _from_tokens(t, like):
        return t.reshape(like.shape)
    x = _L0_conv_ref(x, L0_conv_gamma, L0_conv_beta)
    x = _L1_conv_ref(x, L1_conv_n1_g, L1_conv_n1_b, L1_conv_n2_g, L1_conv_n2_b, L1_conv_w1, L1_conv_b1, L1_conv_w2, L1_conv_b2, L1_conv_mw1, L1_conv_mb1, L1_conv_mw2, L1_conv_mb2)
    return x

_drawn_inputs = setup_inputs


def setup_inputs(seed=0):
    import zlib

    import numpy as np

    out = dict(_drawn_inputs(seed))
    spreads = {'L0_conv_gamma': (1.0, 0.2),
     'L0_conv_beta': (0.0, 0.1),
     'L1_conv_n1_g': (1.0, 0.2),
     'L1_conv_n1_b': (0.0, 0.1),
     'L1_conv_n2_g': (1.0, 0.2),
     'L1_conv_n2_b': (0.0, 0.1),
     'L1_conv_mb1': (0.0, 0.1),
     'L1_conv_mb2': (0.0, 0.1)}
    factors = {'L1_conv_w1': 8.0, 'L1_conv_b1': 8.0, 'L1_conv_w2': 8.0, 'L1_conv_b2': 6.4}
    for name, (base, spread) in spreads.items():
        noise = np.random.default_rng([zlib.crc32(name.encode()), seed]).standard_normal(out[name].shape)
        drawn = base * np.exp(spread * noise) if base else spread * noise
        out[name] = jnp.asarray(drawn.astype(out[name].dtype))
    for name, factor in factors.items():
        out[name] = (out[name] * factor).astype(out[name].dtype)
    return out
```

```python
from contextlib import ExitStack

import numpy as np

import concourse.bass as bass
from concourse import mybir

F32 = mybir.dt.float32
ALU = mybir.AluOpType
ACT = mybir.ActivationFunctionType
AX_X = mybir.AxisListType.X

B, H, W, C = 16, 56, 56, 64
N_TOK = B * H * W
NB = 8
BS = C // NB
HID = 4 * C
KF = H // 2 + 1
PAIRS = B // 2
ROWS = 2 * H
FREE = W * C
WP = W // 2
CH = C // 2
KR = 2 * KF
KHP = (KF + 1) // 2
SPEC = KF * KF
EPS_COV, EPS_LN, LAM = 1e-3, 1e-5, 0.01
QH = HID // 4
SLICES = 7
SW = W // SLICES

S1, S2, L1, L2, INVW, TR, FIN, B_CHUNKS = 0, 8, 16, 24, 32, 40, 56, 64
A_CHUNKS, C_CHUNKS = 14, 42
RING_A, RING_B, RING_C = 2, 4, 2
B_ACT, B_DVE = 40, 24
C_ACT = 35


def b_reader(k):
    if k < L2:
        return "act", k + 1
    if k < INVW:
        return "dve", k - L2 + 1
    if k < TR:
        return "act", 24 + k - INVW + 1
    if k < FIN:
        j = k - TR
        return ("act", 32 + j // 2 + 1) if j % 2 == 0 else ("dve", 8 + j // 2 + 1)
    return "dve", 16 + k - FIN + 1


def c_reader(k):
    if k == 0:
        return "act", 1
    s, j = (k - 1) // 6, (k - 1) % 6
    if s == SLICES - 1:
        return ("act", 1 + 5 * s + j + 1) if j < 4 else ("dve", SLICES)
    return ("act", 1 + 5 * s + j + 1) if j < 5 else ("dve", s + 1)


CONST_COLS = {"f1": 2 * KR, "f2": 4 * KF, "invw": 2 * 224, "invh": ROWS, "mask1": 128, "mask2": 128,
              "halves": 128, "below": C, "ident": 128, "pilot": 128}
PARAM_COLS = {"w1": 256, "w2": 256, "mw1": 4 * 128, "mw2": 4 * 128, "beta": C, "g1": C, "b1": C, "mb2": C,
              "fb2": 256, "gamma": 1, "g2": 1, "b2": 1, "fb1": 2, "mb1": 4}


def offsets(cols):
    at, out = 0, {}
    for name, n in cols.items():
        out[name] = (at, at + n)
        at += n
    return out, at


def build(nc, x, consts, params, out):
    c_at, c_n = offsets(CONST_COLS)
    p_at, p_n = offsets(PARAM_COLS)
    x_v = x.rearrange("(t b) h w c -> t (b h) (w c)", b=2)
    out_v = out.rearrange("(t b) h w c -> t (b h) (w c)", b=2)

    with ExitStack() as ctx:
        def sb(name, shape):
            return ctx.enter_context(nc.sbuf_tensor(name, shape, F32))

        def sem(name):
            return ctx.enter_context(nc.semaphore(name))

        cst = sb("cst", [128, c_n])
        prm = sb("prm", [128, p_n])

        def cc(name, rows=128):
            return cst[0:rows, c_at[name][0]:c_at[name][1]]

        def pp(name, rows=128):
            return prm[0:rows, p_at[name][0]:p_at[name][1]]

        ident = cc("ident")
        wy = sb("wy", [128, 128])
        w1s = sb("w1s", [128, 256])
        w2s = sb("w2s", [128, 256])
        mw1m = sb("mw1m", [128, 512])
        mw1s = sb("mw1s", [128, 512])
        mw2s = sb("mw2s", [128, 512])
        lo = sb("lo", [128, 256])
        hi = sb("hi", [128, 256])
        hbias = sb("hbias", [128, 4])
        negm = sb("negm", [128, 1])
        nhalf = sb("nhalf", [128, W])

        CW = 130
        xin = sb("xin", [ROWS, FREE])
        ybuf = sb("ybuf", [ROWS, FREE])
        hbuf = sb("hbuf", [ROWS, WP * CW])
        rbuf = sb("rbuf", [ROWS, WP * CW])
        fbuf = sb("fbuf", [ROWS, FREE])
        n2 = sb("n2", [ROWS, FREE])
        xT = sb("xT", [128, WP * ROWS])
        u_r = sb("u_r", [128, CH * 2 * KR])
        p_y = sb("p_y", [128, KHP * 256])
        o_g = sb("o_g", [128, FREE])
        n2T = sb("n2T", [128, 4 * ROWS])
        hid = sb("hid", [128, 4, 4 * ROWS])
        oslice = sb("oslice", [ROWS, 2, SW * C])
        clip = sb("clip", [128, 2, 512])
        stats = sb("stats", [ROWS, W, 6])
        small = sb("small", [ROWS, 8, W])

        psum = ctx.enter_context(nc.psum_tensor("psum", [128, 8, 512], F32))

        s_cst, s_prm, s_x0, s_x1 = sem("s_cst"), sem("s_prm"), sem("s_x0"), sem("s_x1")
        s_ones, s_pilot, s_pilot_sb = sem("s_ones"), sem("s_pilot"), sem("s_pilot_sb")
        s_cent, s_gram = sem("s_cent"), sem("s_gram")
        s_dve, s_pe, s_pool = sem("s_dve"), sem("s_pe"), sem("s_pool")

        gram = psum[:, 0, 0:CW]
        pil = psum[:, 1, 0:C]
        row_ps = psum[0:1, 2, 0:C]
        outer_ps = psum[0:C, 3, 0:C]
        mcol_ps = psum[:, 4, 0:1]
        rowk_ps = [psum[0:C, 5 + j, 0:C + 1] for j in range(2)]
        wt_ps = psum[0:C, 7, 0:C]
        hb_ps = psum[:, 4, 8:12]
        pilot = sb("pilot", [128, C])
        gtmp = sb("gtmp", [C, C + 2])
        elim = sb("elim", [C, 2 * C])
        mult = sb("mult", [C, 4])
        rowd = sb("rowd", [1, 4 * C])
        scol = sb("scol", [C, 4])
        ediag = sb("ediag", [C, C])

        DV_COV = 10
        DV_DIAG = DV_COV + 3 * (C - 1) + 2
        DV_W = DV_DIAG + 2

        with nc.Block() as block:
            xbuf = [xin, ybuf]
            cent = [hbuf, rbuf]
            s_x = [s_x0, s_x1]

            @block.sync
            def _(sp):
                sp.dma_start(xin[:], x_v[0]).then_inc(s_x0, 16)
                sp.dma_start(cst[:], consts).then_inc(s_cst, 16)
                sp.dma_start(ybuf[:], x_v[1]).then_inc(s_x1, 16)
                sp.dma_start(prm[:], params).then_inc(s_prm, 16)
                with sp.Fori(1, PAIRS // 2) as i:
                    for j in range(2):
                        sp.wait_ge(s_cent, 2 * i - 1 + j)
                        sp.dma_start(xbuf[j][:], x_v[bass.ds(2 * i + j, 1)].rearrange("o p f -> (o p) f")).then_inc(s_x[j], 16)

            @block.gpsimd
            def _(pool):
                for t in cent:
                    nc.gpsimd.memset(t[:].rearrange("p (w k) -> p w k", k=CW)[:, :, 2 * C:CW], 1.0).then_inc(s_ones, 1)
                nc.gpsimd.memset(nhalf[:], -0.5).then_inc(s_ones, 1)
                nc.gpsimd.memset(wy[:], 0.0).then_inc(s_ones, 1)
                nc.gpsimd.memset(o_g[:], 0.0).then_inc(s_ones, 1)
                nc.gpsimd.memset(u_r[:, KR * W:], 0.0).then_inc(s_ones, 1)
                pool.wait_ge(s_dve, DV_DIAG)
                pool.wait_ge(s_ones, 6)
                nc.gpsimd.tensor_tensor(scol[:, 2:3], scol[:, 1:2], nhalf[0:C, 0:1], ALU.pow).then_inc(s_pool, 1)

            @block.vector
            def _(dve):
                count = [0]

                def link(ins, wait=True):
                    ins.then_inc(s_dve, 1)
                    count[0] += 1
                    if wait:
                        dve.wait_ge(s_dve, count[0])

                dve.wait_ge(s_pilot, 1)
                nc.vector.tensor_copy(pilot[:], pil).then_inc(s_pilot_sb, 1)
                dve.wait_ge(s_pilot_sb, 1)
                dve.wait_ge(s_ones, 2)

                def centre(j, x_count, cent_count):
                    dve.wait_ge(s_x[j], x_count)
                    if cent_count is not None:
                        dve.wait_ge(s_gram, cent_count)
                    nc.vector.tensor_tensor(
                        cent[j][:].rearrange("p (w k) -> p w k", k=CW)[:, :, 0:2 * C].rearrange("p w (t c) -> p w t c", t=2),
                        xbuf[j][:].rearrange("p (w t c) -> p w t c", t=2, c=C),
                        pilot[0:ROWS, :].unsqueeze(1).unsqueeze(1).broadcast_to((ROWS, WP, 2, C)),
                        ALU.subtract).then_inc(s_cent, 1)

                for j in range(2):
                    centre(j, 16, None)
                with dve.Fori(1, PAIRS // 2) as i:
                    for j in range(2):
                        centre(j, 16 * i + 16, 2 * i - 1 + j)

                dve.wait_ge(s_gram, PAIRS)
                link(nc.vector.tensor_copy(gtmp[:], gram[C:2 * C, C:CW]))
                link(nc.vector.tensor_tensor(gtmp[:, 0:C], gram[0:C, 0:C], gtmp[:, 0:C], ALU.add))
                link(nc.vector.tensor_tensor(gtmp[:, C:C + 1], gram[0:C, 2 * C:2 * C + 1], gtmp[:, C:C + 1], ALU.add))
                dve.wait_ge(s_pe, 1)
                link(nc.vector.tensor_scalar(rowd[:, 0:C], row_ps, 1.0 / N_TOK, None, ALU.mult))
                link(nc.vector.scalar_tensor_tensor(
                    rowd[:, 2 * C:3 * C], pilot[0:1, :], -1.0, rowd[:, 0:C], ALU.mult, ALU.subtract))
                link(nc.vector.tensor_copy(rowd[:, 3 * C:4 * C], rowd[:, 2 * C:3 * C]))
                dve.wait_ge(s_pe, 2)
                link(nc.vector.scalar_tensor_tensor(
                    gtmp[:, 0:C], outer_ps, -float(N_TOK), gtmp[:, 0:C], ALU.mult, ALU.add))
                link(nc.vector.tensor_scalar(
                    gtmp[:, 0:C], gtmp[:, 0:C], 1.0 / (N_TOK - 1.0), 1.0 - EPS_COV, ALU.mult, ALU.mult))
                link(nc.vector.tensor_copy(elim[:, C:2 * C], ident[0:C, 0:C]))
                link(nc.vector.scalar_tensor_tensor(
                    elim[:, 0:C], ident[0:C, 0:C], EPS_COV, gtmp[:, 0:C], ALU.mult, ALU.add))
                assert count[0] == DV_COV
                for k in range(C - 1):
                    dve.wait_ge(s_pe, 3 + k + 1)
                    link(nc.vector.reciprocal(mult[:, 0:1], rowk_ps[k % 2][:, 0:1]))
                    link(nc.vector.scalar_tensor_tensor(
                        mult[:, 1:2], elim[:, k:k + 1], mult[:, 0:1], cc("below", C)[:, k:k + 1], ALU.mult, ALU.mult))
                    link(nc.vector.scalar_tensor_tensor(
                        elim[:, k + 1:k + 1 + C], rowk_ps[k % 2][:, 1:C + 1], mult[:, 1:2],
                        elim[:, k + 1:k + 1 + C], ALU.mult, ALU.add))
                link(nc.vector.tensor_tensor(ediag[:], elim[:, 0:C], ident[0:C, 0:C], ALU.mult))
                link(nc.vector.reduce_sum(scol[:, 1:2], ediag[:], AX_X))
                assert count[0] == DV_DIAG
                dve.wait_ge(s_pool, 1)
                dve.wait_ge(s_prm, 16)
                link(nc.vector.tensor_tensor(scol[:, 3:4], scol[:, 2:3], pp("gamma", C), ALU.mult))
                link(nc.vector.tensor_scalar(ediag[:], elim[:, C:2 * C], scol[:, 3:4], None, ALU.mult))
                dve.wait_ge(s_pe, 3 + C - 1 + 1)
                link(nc.vector.tensor_copy(wy[0:C, 0:C], wt_ps))
                link(nc.vector.tensor_copy(wy[C:2 * C, C:2 * C], wt_ps))
                link(nc.vector.tensor_copy(negm[:], mcol_ps))
                for t, src, mask in ((w1s, "w1", "mask1"), (w2s, "w2", "mask2")):
                    for h in range(2):
                        link(nc.vector.tensor_tensor(t[:, 128 * h:128 * h + 128],
                                                     pp(src)[:, 128 * h:128 * h + 128], cc(mask), ALU.mult))
                for t, src in ((mw1m, "mw1"), (mw2s, "mw2")):
                    for q in range(4):
                        link(nc.vector.tensor_tensor(t[:, 128 * q:128 * q + 128],
                                                     pp(src)[:, 128 * q:128 * q + 128], cc("halves"), ALU.mult))
                link(nc.vector.tensor_scalar(mw1s[:], mw1m[:], pp("g2"), None, ALU.mult))
                link(nc.vector.tensor_scalar(lo[:], pp("fb2"), -1.0, -LAM, ALU.mult, ALU.add))
                link(nc.vector.tensor_scalar(hi[:], pp("fb2"), -1.0, LAM, ALU.mult, ALU.add))
                dve.wait_ge(s_pe, 3 + C - 1 + 2)
                link(nc.vector.tensor_tensor(hbias[:], hb_ps, pp("mb1"), ALU.add))

            @block.tensor
            def _(pe):
                pe.wait_ge(s_cst, 16)
                pe.wait_ge(s_x0, 16)
                nc.tensor.matmul(pil, cc("pilot", ROWS), xin[:, 0:C], start=True, stop=True).then_inc(s_pilot, 1)

                def gram_tile(j, count, first):
                    pe.wait_ge(s_cent, count)
                    for w in range(WP):
                        last = nc.tensor.matmul(gram, cent[j][:, w * CW:w * CW + 2 * C], cent[j][:, w * CW:w * CW + CW],
                                                start=(first and w == 0), stop=False, skip_group_check=True)
                    last.then_inc(s_gram, 1)

                gram_tile(0, 1, True)
                gram_tile(1, 2, False)
                with pe.Fori(1, PAIRS // 2) as i:
                    for j in range(2):
                        gram_tile(j, 2 * i + 1 + j, False)
                pe.wait_ge(s_dve, 3)
                nc.tensor.matmul(row_ps, gtmp[:, C:C + 1], ident[0:C, 0:C], start=True, stop=True).then_inc(s_pe, 1)
                pe.wait_ge(s_dve, 4)
                nc.tensor.matmul(outer_ps, rowd[:, 0:C], rowd[:, 0:C], start=True, stop=True).then_inc(s_pe, 1)
                pe.wait_ge(s_dve, 6)
                nc.tensor.matmul(mcol_ps, rowd[:, 2 * C:4 * C], ident[0:1, 0:1], start=True, stop=True).then_inc(s_pe, 1)
                for k in range(C - 1):
                    pe.wait_ge(s_dve, DV_COV + 3 * k)
                    nc.tensor.matmul(rowk_ps[k % 2], ident[0:C, k:k + 1].broadcast_to((C, C)), elim[:, k:k + C + 1],
                                     start=True, stop=True).then_inc(s_pe, 1)
                pe.wait_ge(s_dve, DV_W)
                nc.tensor.transpose(wt_ps, ediag[:], ident[0:C, 0:C]).then_inc(s_pe, 1)
                pe.wait_ge(s_dve, DV_W + 3 + 4 + 4)
                for q in range(4):
                    last = nc.tensor.matmul(hb_ps[:, q:q + 1], mw1m[:, 128 * q:128 * q + 128], pp("b2"),
                                            start=True, stop=True)
                last.then_inc(s_pe, 1)

        x_in, pe_a, pe_b, pe_c = sem("x_in"), sem("pe_a"), sem("pe_b"), sem("pe_c")
        a_act, a_dve = sem("a_act"), sem("a_dve")
        b_act, b_dve = sem("b_act"), sem("b_dve")
        c_act, c_dve = sem("c_act"), sem("c_dve")
        var_ready = [sem("var1_ready"), sem("var2_ready")]
        rstd_ready = [sem("rstd1_ready"), sem("rstd2_ready")]
        ln_step = [sem("ln1_step"), sem("ln2_step")]
        norm_step = [sem("norm1_step"), sem("norm2_step")]
        shrink_step = sem("shrink_step")
        n1_ready, h_step, h_ready, r_ready = sem("n1_ready"), sem("h_step"), sem("h_ready"), sem("r_ready")
        n2_ready, f_biased = sem("n2_ready"), sem("f_biased")
        stored = [sem("stored0"), sem("stored1")]

        ring_a = [psum[:, j, :] for j in range(RING_A)]
        ring_b = [psum[:, RING_A + j, :] for j in range(RING_B)]
        ring_c = [psum[:, RING_A + RING_B + j, :] for j in range(RING_C)]

        u_v = u_r[0:ROWS, :].rearrange("p (m j) -> p m j", j=CH)
        r_v = u_r[:, 0:KF * 112]
        p_v = p_y[:, 0:2 * 2 * SPEC].rearrange("p (b h k w) -> p b h k w", b=2, h=2, k=KF)
        o_v = o_g[:, 0:2 * 2 * SPEC].rearrange("p (h k s w) -> p h s k w", h=2, s=2, k=KF)
        y_v = p_y[:].rearrange("p (k m) -> p k m", m=256)
        h_nat = hbuf[:, 0:FREE]
        r_nat = rbuf[:, 0:FREE]
        h_w = h_nat.rearrange("p (m j) -> p m j", j=CH)

        def bc(ap2, n):
            return ap2.unsqueeze(2).broadcast_to((ROWS, n, C))

        def row(name, n):
            return pp(name, ROWS).unsqueeze(1).broadcast_to((ROWS, n, C))

        def turn_copy(copy, k):
            w0, n = TURN_W[k]
            t = ring_b[k % RING_B][0:KR, 0:n * 128].rearrange("p (w b c) -> p b w c", b=2, c=C)
            g = o_g[:].rearrange("p (w c) -> p w c", c=C)
            for b in range(2):
                last = copy(g[C * b:C * b + KR, w0:w0 + n, :], t[:, b])
            return last

        with nc.Block() as block:

            @block.sync
            def _(sp):
                def load(p):
                    src = x_v[p] if isinstance(p, int) else x_v[bass.ds(p, 1)].rearrange("o p f -> (o p) f")
                    sp.dma_start(xin[:], src).then_inc(x_in, 16)

                def store(p, s):
                    sp.wait_ge(c_dve, p * SLICES + s + 1)
                    o = out_v[p] if isinstance(p, int) else out_v[bass.ds(p, 1)].rearrange("o p f -> (o p) f")
                    sp.dma_start(o[:, s * SW * C:(s + 1) * SW * C], oslice[:, s % 2, :]).then_inc(stored[s % 2], 16)

                load(0)
                sp.wait_ge(pe_a, 7)
                load(1)
                sp.wait_ge(pe_a, A_CHUNKS + 7)
                load(2)
                with sp.Fori(1, PAIRS - 2) as i:
                    sp.wait_ge(pe_a, (i + 1) * A_CHUNKS + 7)
                    load(i + 2)
                    for s in range(SLICES):
                        store(i - 1, s)
                for p in range(PAIRS - 3, PAIRS):
                    for s in range(SLICES):
                        store(p, s)
                sp.wait_ge(stored[0], 16 * 4 * PAIRS)
                sp.wait_ge(stored[1], 16 * 3 * PAIRS)

            @block.tensor
            def _(pe):
                def free_b(i, k):
                    j = k - RING_B
                    if j < 0:
                        if isinstance(i, int) and i == 0:
                            return ring_b[k % RING_B]
                        who, n = b_reader(j + B_CHUNKS)
                        i = i - 1
                    else:
                        who, n = b_reader(j)
                    if who == "act":
                        pe.wait_ge(b_act, i * B_ACT + n)
                    else:
                        pe.wait_ge(b_dve, i * B_DVE + n)
                    return ring_b[k % RING_B]

                def free_c(i, k):
                    j = k - RING_C
                    if j < 0:
                        if isinstance(i, int) and i == 0:
                            return ring_c[k % RING_C]
                        who, n = c_reader(j + C_CHUNKS)
                        i = i - 1
                    else:
                        who, n = c_reader(j)
                    if who == "act":
                        pe.wait_ge(c_act, i * C_ACT + n)
                    else:
                        pe.wait_ge(c_dve, i * SLICES + n)
                    return ring_c[k % RING_C]

                def transpose_x(i):
                    pe.wait_ge(x_in, 16 * i + 16)
                    for k in range(7):
                        if k >= RING_A:
                            pe.wait_ge(a_act, i * 7 + k - RING_A + 1)
                        elif not isinstance(i, int) or i > 0:
                            pe.wait_ge(a_dve, i * 7 - RING_A + k + 1)
                        t = ring_a[k % RING_A]
                        for j in range(4):
                            w = 4 * k + j
                            last = nc.tensor.transpose(t[:, j * ROWS:(j + 1) * ROWS], xin[:, w * 128:w * 128 + 128],
                                                       ident[0:ROWS, 0:ROWS])
                        last.then_inc(pe_a, 1)

                def whiten(i):
                    pe.wait_ge(a_act, i * 7 + 7)
                    for k in range(7):
                        if k + 7 - RING_A >= 7:
                            pe.wait_ge(a_dve, i * 7 + k - RING_A + 1)
                        t = ring_a[(k + 7) % RING_A]
                        for j in range(4):
                            w = 4 * k + j
                            last = nc.tensor.matmul(t[0:ROWS, j * 128:(j + 1) * 128], xT[:, w * ROWS:(w + 1) * ROWS],
                                                    wy[:], start=True, stop=True)
                        last.then_inc(pe_a, 1)

                def dft_h(i):
                    pe.wait_ge(h_ready, i + 1)
                    for k in range(8):
                        t = free_b(i, S1 + k)
                        for j in range(4):
                            last = nc.tensor.matmul(t[0:ROWS, j * 2 * KR:(j + 1) * 2 * KR], h_w[:, :, 4 * k + j],
                                                    cc("f1", ROWS), start=True, stop=True)
                        last.then_inc(pe_b, 1)

                def dft_w(i):
                    pe.wait_ge(b_act, i * B_ACT + S1 + 8)
                    for k in range(8):
                        t = free_b(i, S2 + k)
                        for j in range(min(4, KF - 4 * k)):
                            last = nc.tensor.matmul(t[:, j * 4 * KF:(j + 1) * 4 * KF], u_r[0:ROWS, (4 * k + j) * 128:(4 * k + j + 1) * 128],
                                                    cc("f2", ROWS), start=True, stop=True)
                        last.then_inc(pe_b, 1)

                def layer_1(i):
                    pe.wait_ge(b_act, i * B_ACT + S2 + 8)
                    for k in range(8):
                        half, b, part = k // 4, k // 2 % 2, k % 2
                        t = free_b(i, L1 + k)
                        a, z = L1_PARTS[part]
                        nc.tensor.matmul(t[:, 0:(z - a) * KF], w1s[:, 128 * half:128 * half + 128],
                                         p_v[:, b, half, a:z, :].rearrange("p k w -> p (k w)"),
                                         start=True, stop=True).then_inc(pe_b, 1)

                def layer_2(i, half):
                    pe.wait_ge(b_act, i * B_ACT + L1 + 4 * half + 4)
                    for k in range(4):
                        t = free_b(i, L2 + 4 * half + k)
                        for j in range(min(4, KHP - 4 * k)):
                            kh = 2 * (4 * k + j)
                            n = min(2, KF - kh)
                            lhs = o_g[:, (half * KF + kh) * KR:(half * KF + kh + n) * KR]
                            last = nc.tensor.matmul(t[0:n * KR, j * 128:j * 128 + 128], lhs,
                                                    w2s[:, 128 * half:128 * half + 128], start=True, stop=True)
                        last.then_inc(pe_b, 1)

                def inv_w(i, ks):
                    for k in ks:
                        pe.wait_ge(b_dve, i * B_DVE + 4 + k // 2 + 1)
                        t = free_b(i, INVW + k)
                        for j in range(min(2, KHP - 2 * k)):
                            kp = 2 * k + j
                            n = min(2, KF - 2 * kp)
                            for r in range(2):
                                last = nc.tensor.matmul(t[:, j * 224:j * 224 + n * 112],
                                                        y_v[0:n * KR, kp, 128 * r:128 * r + 128],
                                                        cc("invw", n * KR)[:, 224 * r:224 * r + n * 112],
                                                        start=(r == 0), stop=(r == 1))
                        last.then_inc(pe_b, 1)

                def turn(i, ks):
                    pe.wait_ge(b_act, i * B_ACT + 32)
                    for k in ks:
                        t = free_b(i, TR + k)
                        w0, n = TURN_W[k]
                        for j in range(n):
                            w = w0 + j
                            last = nc.tensor.transpose(t[0:TURN_M, j * 128:j * 128 + 128],
                                                       u_r[:, w:w + W * (TURN_M - 1) + 1:W], ident)
                        last.then_inc(pe_b, 1)

                def inv_h(i):
                    for k in range(8):
                        pe.wait_ge(b_act, i * B_ACT + 32 + k + 1)
                        pe.wait_ge(b_dve, i * B_DVE + 8 + k + 1)
                        t = free_b(i, FIN + k)
                        nc.tensor.matmul(t[0:ROWS, 0:7 * C], cc("invh", GR), o_g[0:GR, k * 7 * C:(k + 1) * 7 * C],
                                         start=True, stop=True).then_inc(pe_b, 1)

                def transpose_n(i, s):
                    k = 0 if s == 0 else 5 + 6 * (s - 1)
                    if s == 0:
                        pe.wait_ge(n2_ready, 2 * i + 1)
                    if s == 3:
                        pe.wait_ge(n2_ready, 2 * i + 2)
                    t = free_c(i, k)
                    for j in range(4):
                        w = 4 * s + j
                        last = nc.tensor.transpose(t[:, j * ROWS:(j + 1) * ROWS], n2[:, w * 128:w * 128 + 128],
                                                   ident[0:ROWS, 0:ROWS])
                    last.then_inc(pe_c, 1)

                def mlp(i, s):
                    pe.wait_ge(c_act, i * C_ACT + (1 if s == 0 else 5 * s + 1))
                    for q in range(4):
                        t = free_c(i, 1 + 6 * s + q)
                        nc.tensor.matmul(t[:, 0:4 * ROWS], mw1s[:, 128 * q:128 * q + 128], n2T[:],
                                         start=True, stop=True).then_inc(pe_c, 1)
                    if s < SLICES - 1:
                        transpose_n(i, s + 1)
                    k = 6 + 6 * s if s < SLICES - 1 else C_CHUNKS - 1
                    t = free_c(i, k)
                    pe.wait_ge(c_act, i * C_ACT + 1 + 5 * s + 4)
                    for j in range(4):
                        for q in range(4):
                            last = nc.tensor.matmul(t[0:ROWS, j * 128:j * 128 + 128], hid[:, q, j * ROWS:(j + 1) * ROWS],
                                                    mw2s[:, 128 * q:128 * q + 128], start=(q == 0), stop=(q == 3))
                    last.then_inc(pe_c, 1)

                def step(i, ahead, behind):
                    dft_h(i)
                    if ahead:
                        transpose_x(i + 1)
                    dft_w(i)
                    layer_1(i)
                    if ahead:
                        whiten(i + 1)
                    if behind:
                        transpose_n(i - 1, 0)
                        mlp(i - 1, 0)
                    layer_2(i, 0)
                    if behind:
                        mlp(i - 1, 1)
                    layer_2(i, 1)
                    if behind:
                        mlp(i - 1, 2)
                    inv_w(i, range(0, 4))
                    if behind:
                        mlp(i - 1, 3)
                    inv_w(i, range(4, 8))
                    if behind:
                        mlp(i - 1, 4)
                    turn(i, range(0, 8))
                    if behind:
                        mlp(i - 1, 5)
                    turn(i, range(8, 16))
                    if behind:
                        mlp(i - 1, 6)
                    inv_h(i)

                transpose_x(0)
                whiten(0)
                step(0, True, False)
                with pe.Fori(1, PAIRS - 1) as i:
                    step(i, True, True)
                step(PAIRS - 1, False, True)
                transpose_n(PAIRS - 1, 0)
                for s in range(SLICES):
                    mlp(PAIRS - 1, s)

            @block.scalar
            def _(act):
                def ev_x(i):
                    for k in range(7):
                        act.wait_ge(pe_a, i * A_CHUNKS + k + 1)
                        nc.scalar.activation(xT[:, k * 4 * ROWS:(k + 1) * 4 * ROWS], ring_a[k % RING_A][:, 0:4 * ROWS],
                                             ACT.Identity, bias=negm[:]).then_inc(a_act, 1)

                def ev_dft_h(i):
                    for k in range(8):
                        act.wait_ge(pe_b, i * B_CHUNKS + S1 + k + 1)
                        nc.scalar.copy(u_v[:, :, 4 * k:4 * k + 4],
                                       ring_b[k % RING_B][0:ROWS, 0:8 * KR].rearrange("p (j m) -> p m j", j=4)
                                       ).then_inc(b_act, 1)

                def ev_dft_w(i):
                    for k in range(8):
                        act.wait_ge(pe_b, i * B_CHUNKS + S2 + k + 1)
                        n = min(4, KF - 4 * k)
                        t = ring_b[k % RING_B][:, 0:n * 4 * KF].rearrange("p (k s h w) -> p s h k w", s=2, h=2, w=KF)
                        for b in range(2):
                            for s in range(2):
                                last = nc.scalar.copy(p_v[C * s:C * s + C, b, :, 4 * k:4 * k + n, :],
                                                      t[C * b:C * b + C, s])
                        last.then_inc(b_act, 1)

                def ev_layer_1(i):
                    for k in range(8):
                        half, b, part = k // 4, k // 2 % 2, k % 2
                        act.wait_ge(pe_b, i * B_CHUNKS + L1 + k + 1)
                        a, z = L1_PARTS[part]
                        t = ring_b[k % RING_B][:, 0:(z - a) * KF]
                        for s in range(2):
                            last = nc.scalar.activation(
                                o_v[C * b:C * b + C, half, s, a:z, :],
                                t[C * s:C * s + C, :].rearrange("p (k w) -> p k w", w=KF), ACT.Relu,
                                bias=pp("fb1")[C * s:C * s + C, half:half + 1])
                        last.then_inc(b_act, 1)

                def ev_inv_w(i, ks):
                    for k in ks:
                        act.wait_ge(pe_b, i * B_CHUNKS + INVW + k + 1)
                        n = min(4, KF - 4 * k) * 112
                        nc.scalar.copy(r_v[:, k * 448:k * 448 + n], ring_b[k % RING_B][:, 0:n]).then_inc(b_act, 1)

                def ev_turn(i, ks):
                    for k in ks:
                        act.wait_ge(pe_b, i * B_CHUNKS + TR + k + 1)
                        turn_copy(nc.scalar.copy, k).then_inc(b_act, 1)

                def ev_n2(i, s):
                    k = 0 if s == 0 else 5 + 6 * (s - 1)
                    act.wait_ge(pe_c, i * C_CHUNKS + k + 1)
                    nc.scalar.copy(n2T[:], ring_c[k % RING_C][:, 0:4 * ROWS]).then_inc(c_act, 1)

                def gelu(i, s):
                    for q in range(4):
                        k = 1 + 6 * s + q
                        act.wait_ge(pe_c, i * C_CHUNKS + k + 1)
                        nc.scalar.activation(hid[:, q, :], ring_c[k % RING_C][:, 0:4 * ROWS], ACT.Gelu,
                                             bias=hbias[:, q:q + 1]).then_inc(c_act, 1)
                    if s < SLICES - 1:
                        ev_n2(i, s + 1)

                def step(i, ahead, behind):
                    ev_dft_h(i)
                    if ahead:
                        ev_x(i + 1)
                    ev_dft_w(i)
                    ev_layer_1(i)
                    if behind:
                        ev_n2(i - 1, 0)
                        gelu(i - 1, 0)
                        gelu(i - 1, 1)
                        gelu(i - 1, 2)
                    ev_inv_w(i, range(0, 4))
                    if behind:
                        gelu(i - 1, 3)
                    ev_inv_w(i, range(4, 8))
                    if behind:
                        gelu(i - 1, 4)
                    ev_turn(i, range(0, 8, 2))
                    if behind:
                        gelu(i - 1, 5)
                    ev_turn(i, range(8, 16, 2))
                    if behind:
                        gelu(i - 1, 6)

                ev_x(0)
                step(0, True, False)
                with act.Fori(1, PAIRS - 1) as i:
                    step(i, True, True)
                step(PAIRS - 1, False, True)
                ev_n2(PAIRS - 1, 0)
                for s in range(SLICES):
                    gelu(PAIRS - 1, s)

            @block.vector
            def _(dve):
                def moments(src, i, ln):
                    at, count = 4 * ln, [0]

                    def link(ins):
                        ins.then_inc(ln_step[ln], 1)
                        count[0] += 1
                        dve.wait_ge(ln_step[ln], i * 7 + count[0])

                    for w in range(W):
                        last = nc.vector.bn_stats(stats[:, w, :], src[:, w * C:(w + 1) * C])
                    link(last)
                    me, ve, mo, vo = (stats[:, :, j] for j in (1, 2, 4, 5))
                    mean, dev, var = small[:, at, :], small[:, at + 1, :], small[:, at + 2, :]
                    link(nc.vector.tensor_tensor(dev, me, mo, ALU.subtract))
                    link(nc.vector.scalar_tensor_tensor(dev, dev, 0.25, dev, ALU.mult, ALU.mult))
                    link(nc.vector.tensor_tensor(var, ve, vo, ALU.add))
                    link(nc.vector.scalar_tensor_tensor(var, var, 1.0 / C, dev, ALU.mult, ALU.add))
                    nc.vector.tensor_scalar(var, var, EPS_LN, None, ALU.add).then_inc(var_ready[ln], 1)
                    link(nc.vector.tensor_tensor(mean, me, mo, ALU.add))
                    link(nc.vector.tensor_scalar(mean, mean, 0.5, None, ALU.mult))

                def normalise(src, dst, i, ln, k):
                    w0, n = k * WP, WP
                    mean, rstd = small[:, 4 * ln, w0:w0 + n], small[:, 4 * ln + 3, w0:w0 + n]
                    s = src[:, w0 * C:(w0 + n) * C].rearrange("p (w c) -> p w c", c=C)
                    d = dst[:, w0 * C:(w0 + n) * C].rearrange("p (w c) -> p w c", c=C)
                    nc.vector.tensor_tensor(d, s, bc(mean, n), ALU.subtract).then_inc(norm_step[ln], 1)
                    dve.wait_ge(norm_step[ln], i * 2 + k + 1)
                    return nc.vector.tensor_tensor(d, d, bc(rstd, n), ALU.mult)

                def ln1_norm(i):
                    dve.wait_ge(rstd_ready[0], i + 1)
                    normalise(ybuf, h_nat, i, 0, 0)
                    normalise(ybuf, h_nat, i, 0, 1).then_inc(n1_ready, 1)

                def ln2(i):
                    moments(fbuf, i, 1)
                    dve.wait_ge(rstd_ready[1], i + 1)
                    for k in range(2):
                        normalise(fbuf, n2, i, 1, k).then_inc(n2_ready, 1)

                def ev_whiten(i):
                    if not isinstance(i, int) or i > 0:
                        dve.wait_ge(r_ready, i)
                    for k in range(7):
                        dve.wait_ge(pe_a, i * A_CHUNKS + 7 + k + 1)
                        nc.vector.tensor_tensor(
                            ybuf[:, k * 512:(k + 1) * 512].rearrange("p (w c) -> p w c", c=C),
                            ring_a[(k + 7) % RING_A][0:ROWS, :].rearrange("p (w c) -> p w c", c=C),
                            row("beta", 8), ALU.add).then_inc(a_dve, 1)

                def shrink(i, half):
                    for k in range(4):
                        c = 4 * half + k
                        dve.wait_ge(pe_b, i * B_CHUNKS + L2 + c + 1)
                        if c >= 2:
                            dve.wait_ge(b_dve, i * B_DVE + c - 1)
                        t = ring_b[c % RING_B]
                        parts = [(2 * KR, 0, 4)] if k < 3 else [(2 * KR, 0, 2), (KR, 2, 3)]
                        for p, (rows, a, z) in enumerate(parts):
                            n = z - a
                            v = t[0:rows, a * 128:z * 128]
                            q = clip[0:rows, k % 2, a * 128:z * 128]
                            lohi = [m[0:rows, 128 * half:128 * half + 128].unsqueeze(1).broadcast_to((rows, n, 128))
                                    for m in (lo, hi)]
                            v3, q3 = (m.rearrange("p (k m) -> p k m", m=128) for m in (v, q))
                            at = 2 * (c + (1 if half == 1 else 0) + p)
                            nc.vector.tensor_tensor(q3, v3, lohi[0], ALU.max).then_inc(shrink_step, 1)
                            dve.wait_ge(shrink_step, i * 20 + at + 1)
                            nc.vector.tensor_tensor(q3, q3, lohi[1], ALU.min).then_inc(shrink_step, 1)
                            dve.wait_ge(shrink_step, i * 20 + at + 2)
                            for r in range(2):
                                yk = y_v[0:rows, 4 * k + a:4 * k + z, 128 * r:128 * r + 128].rearrange(
                                    "p k (b h j) -> p h k b j", b=2, h=2)[:, half]
                                last = nc.vector.tensor_tensor(
                                    yk, v3.rearrange("p k (r b j) -> p r k b j", r=2, b=2)[:, r],
                                    q3.rearrange("p k (r b j) -> p r k b j", r=2, b=2)[:, r], ALU.subtract)
                        last.then_inc(b_dve, 1)

                def ev_mlp(i, s):
                    k = 6 + 6 * s if s < SLICES - 1 else C_CHUNKS - 1
                    dve.wait_ge(pe_c, i * C_CHUNKS + k + 1)
                    if s == 0:
                        dve.wait_ge(f_biased, i + 1)
                    uses = 4 if s % 2 == 0 else 3
                    if s >= 2 or not isinstance(i, int) or i > 0:
                        dve.wait_ge(stored[s % 2], 16 * (i * uses + s // 2))
                    nc.vector.tensor_tensor(oslice[:, s % 2, :], ring_c[k % RING_C][0:ROWS, :],
                                            fbuf[:, s * SW * C:(s + 1) * SW * C], ALU.add).then_inc(c_dve, 1)

                def ev_turn(i, ks):
                    for k in ks:
                        dve.wait_ge(pe_b, i * B_CHUNKS + TR + k + 1)
                        turn_copy(nc.vector.tensor_copy, k).then_inc(b_dve, 1)

                def ev_inv_h(i):
                    dve.wait_ge(r_ready, i + 1)
                    if not isinstance(i, int) or i > 0:
                        dve.wait_ge(c_dve, i * SLICES)
                    for k in range(8):
                        dve.wait_ge(pe_b, i * B_CHUNKS + FIN + k + 1)
                        nc.vector.tensor_tensor(fbuf[:, k * 7 * C:(k + 1) * 7 * C], ring_b[k % RING_B][0:ROWS, 0:7 * C],
                                                r_nat[:, k * 7 * C:(k + 1) * 7 * C], ALU.add).then_inc(b_dve, 1)

                def step(i, ahead, behind):
                    if behind:
                        dve.wait_ge(b_dve, i * B_DVE)
                        ln2(i - 1)
                    if ahead:
                        ev_whiten(i + 1)
                    if behind:
                        ev_mlp(i - 1, 0)
                    shrink(i, 0)
                    if behind:
                        ev_mlp(i - 1, 1)
                    shrink(i, 1)
                    if behind:
                        ev_mlp(i - 1, 2)
                    if ahead:
                        dve.wait_ge(a_dve, (i + 2) * 7)
                        moments(ybuf, i + 1, 0)
                    if behind:
                        ev_mlp(i - 1, 3)
                    if ahead:
                        ln1_norm(i + 1)
                    if behind:
                        ev_mlp(i - 1, 4)
                    ev_turn(i, range(1, 8, 2))
                    if behind:
                        ev_mlp(i - 1, 5)
                    ev_turn(i, range(9, 16, 2))
                    if behind:
                        ev_mlp(i - 1, 6)
                    ev_inv_h(i)

                ev_whiten(0)
                dve.wait_ge(a_dve, 7)
                moments(ybuf, 0, 0)
                ln1_norm(0)
                step(0, True, False)
                with dve.Fori(1, PAIRS - 1) as i:
                    step(i, True, True)
                step(PAIRS - 1, False, True)
                dve.wait_ge(b_dve, PAIRS * B_DVE)
                ln2(PAIRS - 1)
                for s in range(SLICES):
                    ev_mlp(PAIRS - 1, s)

            @block.gpsimd
            def _(pool):
                def rstd(i, ln):
                    pool.wait_ge(var_ready[ln], i + 1)
                    nc.gpsimd.tensor_tensor(small[:, 4 * ln + 3, :], small[:, 4 * ln + 2, :], nhalf[0:ROWS, :],
                                            ALU.pow).then_inc(rstd_ready[ln], 1)

                h3, y3, r3, f3 = (t.rearrange("p (w c) -> p w c", c=C) for t in (h_nat, ybuf[:], r_nat, fbuf[:]))

                def scale_h(i):
                    pool.wait_ge(n1_ready, i + 1)
                    nc.gpsimd.tensor_tensor(h3, h3, row("g1", W), ALU.mult).then_inc(h_step, 1)
                    pool.wait_ge(h_step, i + 1)
                    nc.gpsimd.tensor_tensor(h3, h3, row("b1", W), ALU.add).then_inc(h_ready, 1)

                def residual(i):
                    if not isinstance(i, int) or i > 0:
                        pool.wait_ge(b_dve, i * B_DVE)
                    pool.wait_ge(h_ready, i + 1)
                    nc.gpsimd.tensor_tensor(r3, h3, y3, ALU.add).then_inc(r_ready, 1)

                def bias_f(i):
                    pool.wait_ge(n2_ready, 2 * i + 2)
                    nc.gpsimd.tensor_tensor(f3, f3, row("mb2", W), ALU.add).then_inc(f_biased, 1)

                rstd(0, 0)
                scale_h(0)
                residual(0)
                rstd(1, 0)
                scale_h(1)
                with pool.Fori(1, PAIRS - 1) as i:
                    rstd(i - 1, 1)
                    residual(i)
                    bias_f(i - 1)
                    rstd(i + 1, 0)
                    scale_h(i + 1)
                rstd(PAIRS - 2, 1)
                residual(PAIRS - 1)
                bias_f(PAIRS - 2)
                rstd(PAIRS - 1, 1)
                bias_f(PAIRS - 1)


GR = C + KR
TURN_M = 65
L1_PARTS = [(0, 15), (15, KF)]
TURN_W = [(7 * (k // 2) + (0 if k % 2 == 0 else 4), 4 if k % 2 == 0 else 3) for k in range(16)]


def constants():
    at, n = offsets(CONST_COLS)
    c = np.zeros((128, n), np.float32)

    def put(name, m):
        c[:m.shape[0], at[name][0]:at[name][1]] = m.reshape(m.shape[0], -1)

    pos, k = np.arange(H), np.arange(KF)
    cos = np.cos(2 * np.pi * (np.outer(pos, k) % H) / H)
    sin = np.sin(2 * np.pi * (np.outer(pos, k) % H) / H)
    f1 = np.zeros((2, H, KF, 2, 2))
    for b in range(2):
        f1[b, :, :, b, 0] = cos / H
        f1[b, :, :, b, 1] = -sin / H
    put("f1", f1.reshape(ROWS, -1))
    f2 = np.zeros((W, 2, 2, 2, KF))
    for h in range(2):
        f2[:, h, 0, h, :] = cos
        f2[:, h, 1, h, :] = sin
    put("f2", f2.reshape(ROWS, -1))
    wk = np.where((k == 0) | (k == KF - 1), 0.5, 1.0)
    inv = np.zeros((2, 2, KF, 2, 2, 2, W))
    for q in range(2):
        for s, sign in enumerate((1.0, -1.0)):
            inv[q, s, :, 0, q, 0] = (wk * cos).T
            inv[q, s, :, 0, q, 1] = sign * (wk * sin).T
            inv[q, s, :, 1, q, 0] = -(wk * sin).T
            inv[q, s, :, 1, q, 1] = sign * (wk * cos).T
    put("invw", inv.reshape(2 * KR, -1))
    ih = np.zeros((2, 64, 2, H))
    for b in range(2):
        ih[b, 0:KR:2, b] = (2 * wk * cos).T / H
        ih[b, 1:KR:2, b] = -(2 * wk * sin).T / H
    put("invh", ih.reshape(128, -1))
    same = np.kron(np.eye(CH // BS), np.ones((BS, BS)))
    m1 = np.zeros((2, 2, CH, 2, 2, CH))
    for cs, r in ((0, 0), (0, 1), (1, 0), (1, 1)):
        for s, sign in enumerate((1.0, -1.0)):
            to_re = (cs == r)
            coef = {(0, 0): 1.0, (1, 1): sign, (0, 1): sign, (1, 0): -1.0}[cs, r]
            m1[cs, r, :, s, 0] = same * coef * (1.0 if to_re else -1.0)
            m1[cs, r, :, s, 1] = same * coef
    put("mask1", m1.reshape(128, -1))
    m2 = np.zeros((2, 2, CH, 2, 2, CH))
    for b in range(2):
        for r in range(2):
            m2[b, r, :, 0, b] = same * (1.0 if r == 0 else -1.0)
            m2[b, r, :, 1, b] = same
    put("mask2", m2.reshape(128, -1))
    put("halves", np.kron(np.eye(2), np.ones((64, 64))))
    put("below", -np.tril(np.ones((C, C)), -1))
    put("ident", np.eye(128))
    put("pilot", np.full((ROWS, 128), 1.0 / ROWS))
    return c


def layout(i):
    at, n = offsets(PARAM_COLS)
    p = np.zeros((128, n), np.float32)

    def put(name, m):
        p[:m.shape[0], at[name][0]:at[name][1]] = m.reshape(m.shape[0], -1)

    def rows(v):
        return np.broadcast_to(v.reshape(1, -1), (128, v.size))

    G = CH // BS
    w1 = i["L1_conv_w1"].reshape(2, 2, G, BS, BS)
    w2 = i["L1_conv_w2"].reshape(2, 2, G, BS, BS)
    a = np.zeros((2, 2, G, BS, 2, 2, 2, G, BS), np.float32)
    for cs in range(2):
        for r in range(2):
            for ro in range(2):
                part = ro if cs == r else 1 - ro
                a[cs, r, :, :, :, :, ro] = w1[part].transpose(1, 2, 0, 3)[:, :, :, None, None, :]
    put("w1", a.reshape(128, -1))
    a = np.zeros((2, 2, G, BS, 2, 2, 2, G, BS), np.float32)
    for r in range(2):
        for ro in range(2):
            part = ro if r == 0 else 1 - ro
            a[:, r, :, :, :, ro] = w2[part].transpose(1, 2, 0, 3)[None, :, :, :, None, None, :]
    put("w2", a.reshape(128, -1))
    m = i["L1_conv_mw1"].reshape(1, C, 4, 1, QH)
    put("mw1", np.broadcast_to(m, (2, C, 4, 2, QH)).reshape(128, -1))
    m = i["L1_conv_mw2"].reshape(4, QH, C).transpose(1, 0, 2)[None, :, :, None, :]
    put("mw2", np.broadcast_to(m, (2, QH, 4, 2, C)).reshape(128, -1))
    put("beta", rows(i["L0_conv_beta"]))
    put("g1", rows(i["L1_conv_n1_g"]))
    put("b1", rows(i["L1_conv_n1_b"]))
    put("mb2", rows(i["L1_conv_mb2"]))
    fb2 = i["L1_conv_b2"].reshape(2, 2, CH).transpose(1, 0, 2)
    put("fb2", rows(np.broadcast_to(fb2[:, :, None, :], (2, 2, 2, CH))))
    put("gamma", i["L0_conv_gamma"].reshape(C, 1))
    put("g2", np.tile(i["L1_conv_n2_g"], 2).reshape(128, 1))
    put("b2", np.tile(i["L1_conv_n2_b"], 2).reshape(128, 1))
    fb1 = i["L1_conv_b1"].reshape(2, 2, CH).transpose(0, 2, 1)
    put("fb1", np.broadcast_to(fb1[None], (2, 2, CH, 2)).reshape(128, 2))
    mb1 = i["L1_conv_mb1"].reshape(4, QH).T
    put("mb1", np.broadcast_to(mb1[None], (2, QH, 4)).reshape(128, 4))
    return p


def kernel(**inputs):
    import numpy as _np
    import concourse.bacc as _bacc
    from concourse.bass_utils import run_bass_kernel_spmd as _run

    i = {k: _np.asarray(v) for k, v in inputs.items()}
    arrays = {"x_dram": _np.ascontiguousarray(i["x"]), "consts_dram": constants(), "params_dram": layout(i)}
    nc = _bacc.Bacc("TRN2", target_bir_lowering=False, num_devices=1)
    aps = {k: nc.dram_tensor(k, v.shape, F32, kind="ExternalInput").ap() for k, v in arrays.items()}
    out = nc.dram_tensor("out_dram", (B, H, W, C), F32, kind="ExternalOutput").ap()
    build(nc, aps["x_dram"], aps["consts_dram"], aps["params_dram"], out)
    r = _run(nc, [arrays], core_ids=[0])
    return r.results[0]["out_dram"]
```

```python
from contextlib import ExitStack

import numpy as np

import concourse.bass as bass
from concourse import mybir

F32 = mybir.dt.float32
F32R = mybir.dt.float32r
I32 = mybir.dt.int32
ALU = mybir.AluOpType
ACT = mybir.ActivationFunctionType
AX_X = mybir.AxisListType.X

B, H, W, C = 16, 56, 56, 64
N_TOK = B * H * W
NB = 8
BS = C // NB
HID = 4 * C
KF = H // 2 + 1
PAIRS = B // 2
ROWS = 2 * H
FREE = W * C
WP = W // 2
CH = C // 2
KR = 2 * KF
KHP = (KF + 1) // 2
SPEC = KF * KF
EPS_COV, EPS_LN, LAM = 1e-3, 1e-5, 0.01
HH = HID // 2
RSQRT_GUESS = 1597463007.0
SLICES = 7
SW = W // SLICES

S1, S2, L1, L2, INVW, TR, FIN, B_CHUNKS = 0, 8, 16, 24, 32, 40, 56, 64
A_CHUNKS, C_CHUNKS = 14, 42
RING_A, RING_B, RING_C = 2, 4, 2
B_ACT, B_DVE = 40, 24
C_ACT, C_DVE = 28, 14


def b_reader(k):
    if k < L2:
        return "act", k + 1
    if k < INVW:
        return "dve", k - L2 + 1
    if k < TR:
        return "act", 24 + k - INVW + 1
    if k < FIN:
        j = k - TR
        return ("act", 32 + j // 2 + 1) if j % 2 == 0 else ("dve", 8 + j // 2 + 1)
    return "dve", 16 + k - FIN + 1


def lo_done(s):
    return 1 if s == 0 else 2 * s


def out_done(s):
    return C_DVE if s == SLICES - 1 else 2 * s + 3


def c_reader(k):
    if k == 0:
        return "dve", lo_done(0)
    s, j = (k - 1) // 6, (k - 1) % 6
    if j < 4:
        return "act", 4 * s + j + 1
    if j == 4 and s < SLICES - 1:
        return "dve", lo_done(s + 1)
    return "dve", out_done(s)


CONST_COLS = {"f1": 2 * KR, "f2": 4 * KF, "invw": 2 * 224, "invh": ROWS, "mask1": 128, "mask2": 128,
              "below": C, "ident": 128, "pilot": 128}
PARAM_COLS = {"w1": 256, "w2": 256, "mw1": HID, "mw2": 2 * 128, "beta": C, "g1": C, "b1": C, "mb2": C,
              "fb2": 256, "gamma": 1, "g2": 1, "b2": 1, "fb1": 2, "mb1": 2}


def offsets(cols):
    at, out = 0, {}
    for name, n in cols.items():
        out[name] = (at, at + n)
        at += n
    return out, at


def build(nc, x, consts, params, out):
    c_at, c_n = offsets(CONST_COLS)
    p_at, p_n = offsets(PARAM_COLS)
    x_v = x.rearrange("(t b) h w c -> t (b h) (w c)", b=2)
    out_v = out.rearrange("(t b) h w c -> t (b h) (w c)", b=2)

    with ExitStack() as ctx:
        def sb(name, shape, dtype=F32):
            return ctx.enter_context(nc.sbuf_tensor(name, shape, dtype))

        def sem(name):
            return ctx.enter_context(nc.semaphore(name))

        cst = sb("cst", [128, c_n])
        prm = sb("prm", [128, p_n])

        def cc(name, rows=128):
            return cst[0:rows, c_at[name][0]:c_at[name][1]]

        def pp(name, rows=128):
            return prm[0:rows, p_at[name][0]:p_at[name][1]]

        ident = cc("ident")
        wy = sb("wy", [128, 128])
        w1s = sb("w1s", [128, 256])
        w2s = sb("w2s", [128, 256])
        mw1s = sb("mw1s", [128, HID])
        mw1h = sb("mw1h", [128, HID], F32R)
        mw1l = sb("mw1l", [128, HID], F32R)
        hbias = sb("hbias", [128, 2])
        negm = sb("negm", [128, 1])
        nhalf = sb("nhalf", [128, W])

        CW = 130
        xin = sb("xin", [ROWS, FREE])
        ybuf = sb("ybuf", [ROWS, FREE])
        hbuf = sb("hbuf", [ROWS, WP * CW])
        rbuf = sb("rbuf", [ROWS, WP * CW])
        fbuf = sb("fbuf", [ROWS, FREE])
        n2 = sb("n2", [ROWS, FREE])
        xT = sb("xT", [128, WP * ROWS])
        u_r = sb("u_r", [128, CH * 2 * KR])
        p_y = sb("p_y", [128, KHP * 256])
        o_g = sb("o_g", [128, FREE])
        n2T = sb("n2T", [128, 2, 4 * ROWS], F32R)
        hid = sb("hid", [HH, 2, 2, 4 * ROWS])
        oslice = sb("oslice", [ROWS, 2, SW * C])
        layer2 = sb("layer2", [2 * KR, L2_BUFS, 512])
        over = sb("over", [2 * KR, L2_BUFS, 512])
        under = sb("under", [2 * KR, L2_BUFS, 512])
        neg_lam = sb("neg_lam", [128, 1])
        stats = sb("stats", [ROWS, W, 6])
        small = sb("small", [ROWS, 10, W])

        psum = ctx.enter_context(nc.psum_tensor("psum", [128, 8, 512], F32))

        s_cst, s_prm, s_x0, s_x1 = sem("s_cst"), sem("s_prm"), sem("s_x0"), sem("s_x1")
        s_ones, s_pilot, s_pilot_sb = sem("s_ones"), sem("s_pilot"), sem("s_pilot_sb")
        s_cent, s_gram = sem("s_cent"), sem("s_gram")
        s_dve, s_pe, s_pool = sem("s_dve"), sem("s_pe"), sem("s_pool")

        gram = psum[:, 0, 0:CW]
        pil = psum[:, 1, 0:C]
        row_ps = psum[0:1, 2, 0:C]
        outer_ps = psum[0:C, 3, 0:C]
        mcol_ps = psum[:, 4, 0:1]
        rowk_ps = [psum[0:C, 5 + j, 0:C + 1] for j in range(2)]
        wt_ps = psum[0:C, 7, 0:C]
        hb_ps = psum[:, 4, 8:10]
        pilot = sb("pilot", [128, C])
        gtmp = sb("gtmp", [C, C + 2])
        elim = sb("elim", [C, 2 * C])
        mult = sb("mult", [C, 4])
        rowd = sb("rowd", [1, 4 * C])
        scol = sb("scol", [C, 4])
        ediag = sb("ediag", [C, C])

        DV_COV = 10
        DV_DIAG = DV_COV + 3 * (C - 1) + 2
        DV_W = DV_DIAG + 2

        with nc.Block() as block:
            xbuf = [xin, ybuf]
            cent = [hbuf, rbuf]
            s_x = [s_x0, s_x1]

            @block.sync
            def _(sp):
                sp.dma_start(xin[:], x_v[0]).then_inc(s_x0, 16)
                sp.dma_start(cst[:], consts).then_inc(s_cst, 16)
                sp.dma_start(ybuf[:], x_v[1]).then_inc(s_x1, 16)
                sp.dma_start(prm[:], params).then_inc(s_prm, 16)
                with sp.Fori(1, PAIRS // 2) as i:
                    for j in range(2):
                        sp.wait_ge(s_cent, 2 * i - 1 + j)
                        sp.dma_start(xbuf[j][:], x_v[bass.ds(2 * i + j, 1)].rearrange("o p f -> (o p) f")).then_inc(s_x[j], 16)

            @block.gpsimd
            def _(pool):
                for t in cent:
                    nc.gpsimd.memset(t[:].rearrange("p (w k) -> p w k", k=CW)[:, :, 2 * C:CW], 1.0).then_inc(s_ones, 1)
                nc.gpsimd.memset(nhalf[:], -0.5).then_inc(s_ones, 1)
                nc.gpsimd.memset(neg_lam[:], -LAM).then_inc(s_ones, 1)
                nc.gpsimd.memset(wy[:], 0.0).then_inc(s_ones, 1)
                nc.gpsimd.memset(o_g[:], 0.0).then_inc(s_ones, 1)
                nc.gpsimd.memset(u_r[:, KR * W:], 0.0).then_inc(s_ones, 1)
                pool.wait_ge(s_dve, DV_DIAG)
                pool.wait_ge(s_ones, 7)
                nc.gpsimd.tensor_tensor(scol[:, 2:3], scol[:, 1:2], nhalf[0:C, 0:1], ALU.pow).then_inc(s_pool, 1)

            @block.vector
            def _(dve):
                count = [0]

                def link(ins, wait=True):
                    ins.then_inc(s_dve, 1)
                    count[0] += 1
                    if wait:
                        dve.wait_ge(s_dve, count[0])

                dve.wait_ge(s_pilot, 1)
                nc.vector.tensor_copy(pilot[:], pil).then_inc(s_pilot_sb, 1)
                dve.wait_ge(s_pilot_sb, 1)
                dve.wait_ge(s_ones, 2)

                def centre(j, x_count, cent_count):
                    dve.wait_ge(s_x[j], x_count)
                    if cent_count is not None:
                        dve.wait_ge(s_gram, cent_count)
                    nc.vector.tensor_tensor(
                        cent[j][:].rearrange("p (w k) -> p w k", k=CW)[:, :, 0:2 * C].rearrange("p w (t c) -> p w t c", t=2),
                        xbuf[j][:].rearrange("p (w t c) -> p w t c", t=2, c=C),
                        pilot[0:ROWS, :].unsqueeze(1).unsqueeze(1).broadcast_to((ROWS, WP, 2, C)),
                        ALU.subtract).then_inc(s_cent, 1)

                for j in range(2):
                    centre(j, 16, None)
                with dve.Fori(1, PAIRS // 2) as i:
                    for j in range(2):
                        centre(j, 16 * i + 16, 2 * i - 1 + j)

                dve.wait_ge(s_gram, PAIRS)
                link(nc.vector.tensor_copy(gtmp[:], gram[C:2 * C, C:CW]))
                link(nc.vector.tensor_tensor(gtmp[:, 0:C], gram[0:C, 0:C], gtmp[:, 0:C], ALU.add))
                link(nc.vector.tensor_tensor(gtmp[:, C:C + 1], gram[0:C, 2 * C:2 * C + 1], gtmp[:, C:C + 1], ALU.add))
                dve.wait_ge(s_pe, 1)
                link(nc.vector.tensor_scalar(rowd[:, 0:C], row_ps, 1.0 / N_TOK, None, ALU.mult))
                link(nc.vector.scalar_tensor_tensor(
                    rowd[:, 2 * C:3 * C], pilot[0:1, :], -1.0, rowd[:, 0:C], ALU.mult, ALU.subtract))
                link(nc.vector.tensor_copy(rowd[:, 3 * C:4 * C], rowd[:, 2 * C:3 * C]))
                dve.wait_ge(s_pe, 2)
                link(nc.vector.scalar_tensor_tensor(
                    gtmp[:, 0:C], outer_ps, -float(N_TOK), gtmp[:, 0:C], ALU.mult, ALU.add))
                link(nc.vector.tensor_scalar(
                    gtmp[:, 0:C], gtmp[:, 0:C], 1.0 / (N_TOK - 1.0), 1.0 - EPS_COV, ALU.mult, ALU.mult))
                link(nc.vector.tensor_copy(elim[:, C:2 * C], ident[0:C, 0:C]))
                link(nc.vector.scalar_tensor_tensor(
                    elim[:, 0:C], ident[0:C, 0:C], EPS_COV, gtmp[:, 0:C], ALU.mult, ALU.add))
                assert count[0] == DV_COV
                for k in range(C - 1):
                    dve.wait_ge(s_pe, 3 + k + 1)
                    link(nc.vector.reciprocal(mult[:, 0:1], rowk_ps[k % 2][:, 0:1]))
                    link(nc.vector.scalar_tensor_tensor(
                        mult[:, 1:2], elim[:, k:k + 1], mult[:, 0:1], cc("below", C)[:, k:k + 1], ALU.mult, ALU.mult))
                    link(nc.vector.scalar_tensor_tensor(
                        elim[:, k + 1:k + 1 + C], rowk_ps[k % 2][:, 1:C + 1], mult[:, 1:2],
                        elim[:, k + 1:k + 1 + C], ALU.mult, ALU.add))
                link(nc.vector.tensor_tensor(ediag[:], elim[:, 0:C], ident[0:C, 0:C], ALU.mult))
                link(nc.vector.reduce_sum(scol[:, 1:2], ediag[:], AX_X))
                assert count[0] == DV_DIAG
                dve.wait_ge(s_pool, 1)
                dve.wait_ge(s_prm, 16)
                link(nc.vector.tensor_tensor(scol[:, 3:4], scol[:, 2:3], pp("gamma", C), ALU.mult))
                link(nc.vector.tensor_scalar(ediag[:], elim[:, C:2 * C], scol[:, 3:4], None, ALU.mult))
                dve.wait_ge(s_pe, 3 + C - 1 + 1)
                link(nc.vector.tensor_copy(wy[0:C, 0:C], wt_ps))
                link(nc.vector.tensor_copy(wy[C:2 * C, C:2 * C], wt_ps))
                link(nc.vector.tensor_copy(negm[:], mcol_ps))
                for t, src, mask in ((w1s, "w1", "mask1"), (w2s, "w2", "mask2")):
                    for h in range(2):
                        link(nc.vector.tensor_tensor(t[:, 128 * h:128 * h + 128],
                                                     pp(src)[:, 128 * h:128 * h + 128], cc(mask), ALU.mult))
                link(nc.vector.tensor_scalar(mw1s[:], pp("mw1"), pp("g2"), None, ALU.mult))
                link(nc.vector.tensor_copy(mw1h[:], mw1s[:]))
                link(nc.vector.tensor_tensor(mw1l[:], mw1s[:], mw1h[:].bitcast(F32), ALU.subtract))
                dve.wait_ge(s_pe, 3 + C - 1 + 2)
                link(nc.vector.tensor_tensor(hbias[:], hb_ps, pp("mb1"), ALU.add))

            @block.tensor
            def _(pe):
                pe.wait_ge(s_cst, 16)
                pe.wait_ge(s_x0, 16)
                nc.tensor.matmul(pil, cc("pilot", ROWS), xin[:, 0:C], start=True, stop=True).then_inc(s_pilot, 1)

                def gram_tile(j, count, first):
                    pe.wait_ge(s_cent, count)
                    for w in range(WP):
                        last = nc.tensor.matmul(gram, cent[j][:, w * CW:w * CW + 2 * C], cent[j][:, w * CW:w * CW + CW],
                                                start=(first and w == 0), stop=False, skip_group_check=True)
                    last.then_inc(s_gram, 1)

                gram_tile(0, 1, True)
                gram_tile(1, 2, False)
                with pe.Fori(1, PAIRS // 2) as i:
                    for j in range(2):
                        gram_tile(j, 2 * i + 1 + j, False)
                pe.wait_ge(s_dve, 3)
                nc.tensor.matmul(row_ps, gtmp[:, C:C + 1], ident[0:C, 0:C], start=True, stop=True).then_inc(s_pe, 1)
                pe.wait_ge(s_dve, 4)
                nc.tensor.matmul(outer_ps, rowd[:, 0:C], rowd[:, 0:C], start=True, stop=True).then_inc(s_pe, 1)
                pe.wait_ge(s_dve, 6)
                nc.tensor.matmul(mcol_ps, rowd[:, 2 * C:4 * C], ident[0:1, 0:1], start=True, stop=True).then_inc(s_pe, 1)
                for k in range(C - 1):
                    pe.wait_ge(s_dve, DV_COV + 3 * k)
                    nc.tensor.matmul(rowk_ps[k % 2], ident[0:C, k:k + 1].broadcast_to((C, C)), elim[:, k:k + C + 1],
                                     start=True, stop=True).then_inc(s_pe, 1)
                pe.wait_ge(s_dve, DV_W)
                nc.tensor.transpose(wt_ps, ediag[:], ident[0:C, 0:C]).then_inc(s_pe, 1)
                pe.wait_ge(s_prm, 16)
                pe.wait_ge(s_dve, DV_W + 3)
                for m in range(2):
                    last = nc.tensor.matmul(hb_ps[:, m:m + 1], pp("mw1", C)[:, HH * m:HH * m + HH], pp("b2", C),
                                            start=True, stop=True)
                last.then_inc(s_pe, 1)

        x_in, pe_a, pe_b, pe_c = sem("x_in"), sem("pe_a"), sem("pe_b"), sem("pe_c")
        a_act, a_dve = sem("a_act"), sem("a_dve")
        b_act, b_dve = sem("b_act"), sem("b_dve")
        c_act, c_dve = sem("c_act"), sem("c_dve")
        ln_step = [sem("ln1_step"), sem("ln2_step")]
        norm_step = [sem("norm1_step"), sem("norm2_step")]
        shrunk, y_ready = sem("shrunk"), sem("y_ready")
        n1_ready, h_step, h_ready, r_ready = sem("n1_ready"), sem("h_step"), sem("h_ready"), sem("r_ready")
        n2_ready, f_biased, hi_ready = sem("n2_ready"), sem("f_biased"), sem("hi_ready")
        stored = [sem("stored0"), sem("stored1")]

        ring_a = [psum[:, j, :] for j in range(RING_A)]
        ring_b = [psum[:, RING_A + j, :] for j in range(RING_B)]
        ring_c = [psum[:, RING_A + RING_B + j, :] for j in range(RING_C)]

        u_v = u_r[0:ROWS, :].rearrange("p (m j) -> p m j", j=CH)
        r_v = u_r[:, 0:KF * 112]
        p_v = p_y[:, 0:2 * 2 * SPEC].rearrange("p (b h k w) -> p b h k w", b=2, h=2, k=KF)
        o_v = o_g[:, 0:2 * 2 * SPEC].rearrange("p (h k s w) -> p h s k w", h=2, s=2, k=KF)
        y_v = p_y[:].rearrange("p (k m) -> p k m", m=256)
        h_nat = hbuf[:, 0:FREE]
        r_nat = rbuf[:, 0:FREE]
        h_w = h_nat.rearrange("p (m j) -> p m j", j=CH)

        def bc(ap2, n):
            return ap2.unsqueeze(2).broadcast_to((ROWS, n, C))

        def row(name, n):
            return pp(name, ROWS).unsqueeze(1).broadcast_to((ROWS, n, C))

        def turn_copy(copy, k):
            w0, n = TURN_W[k]
            t = ring_b[k % RING_B][0:KR, 0:n * 128].rearrange("p (w b c) -> p b w c", b=2, c=C)
            g = o_g[:].rearrange("p (w c) -> p w c", c=C)
            for b in range(2):
                last = copy(g[C * b:C * b + KR, w0:w0 + n, :], t[:, b])
            return last

        with nc.Block() as block:

            @block.sync
            def _(sp):
                def load(p):
                    src = x_v[p] if isinstance(p, int) else x_v[bass.ds(p, 1)].rearrange("o p f -> (o p) f")
                    sp.dma_start(xin[:], src).then_inc(x_in, 16)

                def store(p, s):
                    sp.wait_ge(c_dve, p * C_DVE + out_done(s))
                    o = out_v[p] if isinstance(p, int) else out_v[bass.ds(p, 1)].rearrange("o p f -> (o p) f")
                    sp.dma_start(o[:, s * SW * C:(s + 1) * SW * C], oslice[:, s % 2, :]).then_inc(stored[s % 2], 16)

                load(0)
                sp.wait_ge(pe_a, 7)
                load(1)
                sp.wait_ge(pe_a, A_CHUNKS + 7)
                load(2)
                with sp.Fori(1, PAIRS - 2) as i:
                    sp.wait_ge(pe_a, (i + 1) * A_CHUNKS + 7)
                    load(i + 2)
                    for s in range(SLICES):
                        store(i - 1, s)
                for p in range(PAIRS - 3, PAIRS):
                    for s in range(SLICES):
                        store(p, s)
                sp.wait_ge(stored[0], 16 * 4 * PAIRS)
                sp.wait_ge(stored[1], 16 * 3 * PAIRS)

            @block.tensor
            def _(pe):
                def free_b(i, k):
                    j = k - RING_B
                    if j < 0:
                        if isinstance(i, int) and i == 0:
                            return ring_b[k % RING_B]
                        who, n = b_reader(j + B_CHUNKS)
                        i = i - 1
                    else:
                        who, n = b_reader(j)
                    if who == "act":
                        pe.wait_ge(b_act, i * B_ACT + n)
                    else:
                        pe.wait_ge(b_dve, i * B_DVE + n)
                    return ring_b[k % RING_B]

                def free_c(i, k):
                    j = k - RING_C
                    if j < 0:
                        if isinstance(i, int) and i == 0:
                            return ring_c[k % RING_C]
                        who, n = c_reader(j + C_CHUNKS)
                        i = i - 1
                    else:
                        who, n = c_reader(j)
                    if who == "act":
                        pe.wait_ge(c_act, i * C_ACT + n)
                    else:
                        pe.wait_ge(c_dve, i * C_DVE + n)
                    return ring_c[k % RING_C]

                def transpose_x(i, ks):
                    if 0 in ks:
                        pe.wait_ge(x_in, 16 * i + 16)
                    for k in ks:
                        if k >= RING_A:
                            pe.wait_ge(a_act, i * 7 + k - RING_A + 1)
                        elif not isinstance(i, int) or i > 0:
                            pe.wait_ge(a_dve, i * 7 - RING_A + k + 1)
                        t = ring_a[k % RING_A]
                        for j in range(4):
                            w = 4 * k + j
                            last = nc.tensor.transpose(t[:, j * ROWS:(j + 1) * ROWS], xin[:, w * 128:w * 128 + 128],
                                                       ident[0:ROWS, 0:ROWS])
                        last.then_inc(pe_a, 1)

                def whiten(i, ks):
                    pe.wait_ge(a_act, i * 7 + 7)
                    for k in ks:
                        if k + 7 - RING_A >= 7:
                            pe.wait_ge(a_dve, i * 7 + k - RING_A + 1)
                        t = ring_a[(k + 7) % RING_A]
                        for j in range(4):
                            w = 4 * k + j
                            last = nc.tensor.matmul(t[0:ROWS, j * 128:(j + 1) * 128], xT[:, w * ROWS:(w + 1) * ROWS],
                                                    wy[:], start=True, stop=True)
                        last.then_inc(pe_a, 1)

                def dft_h(i):
                    pe.wait_ge(h_ready, i + 1)
                    for k in range(8):
                        t = free_b(i, S1 + k)
                        for j in range(4):
                            last = nc.tensor.matmul(t[0:ROWS, j * 2 * KR:(j + 1) * 2 * KR], h_w[:, :, 4 * k + j],
                                                    cc("f1", ROWS), start=True, stop=True)
                        last.then_inc(pe_b, 1)

                def dft_w(i):
                    pe.wait_ge(b_act, i * B_ACT + S1 + 8)
                    for k in range(8):
                        t = free_b(i, S2 + k)
                        for j in range(min(4, KF - 4 * k)):
                            last = nc.tensor.matmul(t[:, j * 4 * KF:(j + 1) * 4 * KF], u_r[0:ROWS, (4 * k + j) * 128:(4 * k + j + 1) * 128],
                                                    cc("f2", ROWS), start=True, stop=True)
                        last.then_inc(pe_b, 1)

                def layer_1(i):
                    for k in range(8):
                        part, half, b = k // 4, k // 2 % 2, k % 2
                        pe.wait_ge(b_act, i * B_ACT + S2 + (4 if part == 0 else 8))
                        t = free_b(i, L1 + k)
                        a, z = L1_PARTS[part]
                        nc.tensor.matmul(t[:, 0:(z - a) * KF], w1s[:, 128 * half:128 * half + 128],
                                         p_v[:, b, half, a:z, :].rearrange("p k w -> p (k w)"),
                                         start=True, stop=True).then_inc(pe_b, 1)

                def layer_2(i, half, k):
                    if half == 0 and k == 0:
                        pe.wait_ge(b_act, i * B_ACT + L1 + 8)
                    t = free_b(i, L2 + 4 * half + k)
                    for j in range(L2_KP[k]):
                        kh = 2 * (4 * k + j)
                        last = nc.tensor.matmul(t[0:2 * KR, j * 128:j * 128 + 128],
                                                o_g[:, (half * KF + kh) * KR:(half * KF + kh + 2) * KR],
                                                w2s[:, 128 * half:128 * half + 128], start=True, stop=True)
                    last.then_inc(pe_b, 1)

                def inv_w(i, ks):
                    for k in ks:
                        pe.wait_ge(y_ready, i * 8 + 4 + k // 2 + 1)
                        t = free_b(i, INVW + k)
                        for j in range(min(2, KHP - 2 * k)):
                            kp = 2 * k + j
                            n = min(2, KF - 2 * kp)
                            for r in range(2):
                                last = nc.tensor.matmul(t[:, j * 224:j * 224 + n * 112],
                                                        y_v[0:n * KR, kp, 128 * r:128 * r + 128],
                                                        cc("invw", n * KR)[:, 224 * r:224 * r + n * 112],
                                                        start=(r == 0), stop=(r == 1))
                        last.then_inc(pe_b, 1)

                def turn(i, ks):
                    pe.wait_ge(b_act, i * B_ACT + 32)
                    for k in ks:
                        t = free_b(i, TR + k)
                        w0, n = TURN_W[k]
                        for j in range(n):
                            w = w0 + j
                            last = nc.tensor.transpose(t[0:TURN_M, j * 128:j * 128 + 128],
                                                       u_r[:, w:w + W * (TURN_M - 1) + 1:W], ident)
                        last.then_inc(pe_b, 1)

                def inv_h(i):
                    for k in range(8):
                        pe.wait_ge(b_act, i * B_ACT + 32 + k + 1)
                        pe.wait_ge(b_dve, i * B_DVE + 8 + k + 1)
                        t = free_b(i, FIN + k)
                        nc.tensor.matmul(t[0:ROWS, 0:7 * C], cc("invh", GR), o_g[0:GR, k * 7 * C:(k + 1) * 7 * C],
                                         start=True, stop=True).then_inc(pe_b, 1)

                def transpose_n(i, s):
                    k = 0 if s == 0 else 5 + 6 * (s - 1)
                    if s == 0:
                        pe.wait_ge(n2_ready, 2 * i + 1)
                    if s == 3:
                        pe.wait_ge(n2_ready, 2 * i + 2)
                    t = free_c(i, k)
                    for j in range(4):
                        w = 4 * s + j
                        last = nc.tensor.transpose(t[:, j * ROWS:(j + 1) * ROWS], n2[:, w * 128:w * 128 + 128],
                                                   ident[0:ROWS, 0:ROWS])
                    last.then_inc(pe_c, 1)

                def mlp(i, s, fill):
                    pe.wait_ge(c_dve, i * C_DVE + lo_done(s))
                    for v in range(2):
                        for m in range(2):
                            if m == 1:
                                fill(v)
                            t = free_c(i, 1 + 6 * s + 2 * v + m)
                            for wt, p in ((mw1h, 0), (mw1l, 1)):
                                last = nc.tensor.matmul(t[:, 0:4 * ROWS], wt[:, HH * m:HH * m + HH], n2T[:, v, :],
                                                        start=(p == 0), stop=(p == 1))
                            last.then_inc(pe_c, 1)
                    fill(2)
                    if s < SLICES - 1:
                        transpose_n(i, s + 1)
                    fill(3)
                    k = 6 + 6 * s if s < SLICES - 1 else C_CHUNKS - 1
                    t = free_c(i, k)
                    pe.wait_ge(c_act, i * C_ACT + 4 * s + 4)
                    for w in range(SW):
                        at, zeros = (w * C, 32) if w < SW - 1 else (w * C - 32, 0)
                        for m in range(2):
                            last = nc.tensor.matmul(t[0:ROWS, at:at + 96],
                                                    hid[:, m, w % 2, (w // 2) * ROWS:(w // 2 + 1) * ROWS],
                                                    pp("mw2")[:, 128 * m + zeros:128 * m + zeros + 96],
                                                    start=(w == 0 and m == 0), stop=(w == SW - 1 and m == 1),
                                                    skip_group_check=True)
                    last.then_inc(pe_c, 1)

                def step(i, ahead, ahead2, behind):
                    def slice_(s, fill):
                        if behind:
                            mlp(i - 1, s, fill)
                        else:
                            for j in range(4):
                                fill(j)

                    def whiten_next(j):
                        if ahead and j < 3:
                            whiten(i + 1, [4 + j])

                    def layer_2_and_x(j):
                        layer_2(i, 0, j)
                        if ahead2:
                            transpose_x(i + 2, range(7)[2 * j:2 * j + 2])

                    dft_h(i)
                    dft_w(i)
                    layer_1(i)
                    if behind:
                        transpose_n(i - 1, 0)
                    if ahead:
                        whiten(i + 1, range(4))
                    slice_(0, whiten_next)
                    slice_(1, layer_2_and_x)
                    slice_(2, lambda j: layer_2(i, 1, j))
                    slice_(3, lambda j: inv_w(i, [j]))
                    slice_(4, lambda j: inv_w(i, [4 + j]))
                    slice_(5, lambda j: turn(i, range(2 * j, 2 * j + 2)))
                    slice_(6, lambda j: turn(i, range(8 + 2 * j, 10 + 2 * j)))
                    inv_h(i)

                transpose_x(0, range(7))
                whiten(0, range(7))
                transpose_x(1, range(7))
                step(0, True, True, False)
                with pe.Fori(1, PAIRS - 2) as i:
                    step(i, True, True, True)
                step(PAIRS - 2, True, False, True)
                step(PAIRS - 1, False, False, True)
                transpose_n(PAIRS - 1, 0)
                for s in range(SLICES):
                    mlp(PAIRS - 1, s, lambda j: None)

            @block.scalar
            def _(act):
                def ev_x(i, ks):
                    for k in ks:
                        act.wait_ge(pe_a, i * A_CHUNKS + k + 1)
                        nc.scalar.activation(xT[:, k * 4 * ROWS:(k + 1) * 4 * ROWS], ring_a[k % RING_A][:, 0:4 * ROWS],
                                             ACT.Identity, bias=negm[:]).then_inc(a_act, 1)

                def ev_dft_h(i):
                    for k in range(8):
                        act.wait_ge(pe_b, i * B_CHUNKS + S1 + k + 1)
                        nc.scalar.copy(u_v[:, :, 4 * k:4 * k + 4],
                                       ring_b[k % RING_B][0:ROWS, 0:8 * KR].rearrange("p (j m) -> p m j", j=4)
                                       ).then_inc(b_act, 1)

                def ev_dft_w(i):
                    for k in range(8):
                        act.wait_ge(pe_b, i * B_CHUNKS + S2 + k + 1)
                        n = min(4, KF - 4 * k)
                        t = ring_b[k % RING_B][:, 0:n * 4 * KF].rearrange("p (k s h w) -> p s h k w", s=2, h=2, w=KF)
                        for b in range(2):
                            for s in range(2):
                                last = nc.scalar.copy(p_v[C * s:C * s + C, b, :, 4 * k:4 * k + n, :],
                                                      t[C * b:C * b + C, s])
                        last.then_inc(b_act, 1)

                def ev_layer_1(i):
                    for k in range(8):
                        part, half, b = k // 4, k // 2 % 2, k % 2
                        act.wait_ge(pe_b, i * B_CHUNKS + L1 + k + 1)
                        a, z = L1_PARTS[part]
                        t = ring_b[k % RING_B][:, 0:(z - a) * KF]
                        for s in range(2):
                            last = nc.scalar.activation(
                                o_v[C * b:C * b + C, half, s, a:z, :],
                                t[C * s:C * s + C, :].rearrange("p (k w) -> p k w", w=KF), ACT.Relu,
                                bias=pp("fb1")[C * s:C * s + C, half:half + 1])
                        last.then_inc(b_act, 1)

                def ev_inv_w(i, ks):
                    for k in ks:
                        act.wait_ge(pe_b, i * B_CHUNKS + INVW + k + 1)
                        n = min(4, KF - 4 * k) * 112
                        nc.scalar.copy(r_v[:, k * 448:k * 448 + n], ring_b[k % RING_B][:, 0:n]).then_inc(b_act, 1)

                def ev_turn(i, ks):
                    for k in ks:
                        act.wait_ge(pe_b, i * B_CHUNKS + TR + k + 1)
                        turn_copy(nc.scalar.copy, k).then_inc(b_act, 1)

                def ev_n2(i, s):
                    k = 0 if s == 0 else 5 + 6 * (s - 1)
                    act.wait_ge(pe_c, i * C_CHUNKS + k + 1)
                    for v in range(2):
                        nc.scalar.copy(n2T[C * v:C * v + C, v, :],
                                       ring_c[k % RING_C][C * v:C * v + C, 0:4 * ROWS]).then_inc(hi_ready, 1)

                def gelu(i, s, fill):
                    for q in range(4):
                        k = 1 + 6 * s + q
                        act.wait_ge(pe_c, i * C_CHUNKS + k + 1)
                        nc.scalar.activation(hid[:, q % 2, q // 2, :], ring_c[k % RING_C][:, 0:4 * ROWS], ACT.Gelu,
                                             bias=hbias[:, q % 2:q % 2 + 1]).then_inc(c_act, 1)
                        if q % 2 == 0:
                            fill(q // 2)
                    fill(2)
                    if s < SLICES - 1:
                        ev_n2(i, s + 1)
                    fill(3)

                def shrink(i, c):
                    n = L2_KP[c % 4] * 128
                    v = layer2[:, c % L2_BUFS, 0:n]
                    act.wait_ge(b_dve, i * B_DVE + c + 1)
                    if c >= L2_BUFS or not isinstance(i, int) or i > 0:
                        act.wait_ge(y_ready, i * 8 + c - L2_BUFS + 1)
                    nc.scalar.activation(over[:, c % L2_BUFS, 0:n], v, ACT.Relu, bias=neg_lam[0:2 * KR, :])
                    nc.scalar.activation(under[:, c % L2_BUFS, 0:n], v, ACT.Relu, bias=neg_lam[0:2 * KR, :],
                                         scale=-1.0).then_inc(shrunk, 1)

                def step(i, ahead2, behind):
                    def slice_(s, fill):
                        if behind:
                            gelu(i - 1, s, fill)
                        else:
                            for j in range(4):
                                fill(j)

                    def x_next(j):
                        if ahead2:
                            ev_x(i + 2, range(7)[2 * j:2 * j + 2])
                        shrink(i, j)

                    def shrink_late(j):
                        if j > 0:
                            shrink(i, 3 + j)

                    def first_inv_w(j):
                        if j == 0:
                            shrink(i, 7)
                        ev_inv_w(i, [j])

                    ev_dft_h(i)
                    ev_dft_w(i)
                    ev_layer_1(i)
                    if behind:
                        ev_n2(i - 1, 0)
                    slice_(0, lambda j: None)
                    slice_(1, x_next)
                    slice_(2, shrink_late)
                    slice_(3, first_inv_w)
                    slice_(4, lambda j: ev_inv_w(i, [4 + j]))
                    slice_(5, lambda j: ev_turn(i, [2 * j]))
                    slice_(6, lambda j: ev_turn(i, [8 + 2 * j]))

                ev_x(0, range(7))
                ev_x(1, range(7))
                step(0, True, False)
                with act.Fori(1, PAIRS - 2) as i:
                    step(i, True, True)
                step(PAIRS - 2, False, True)
                step(PAIRS - 1, False, True)
                ev_n2(PAIRS - 1, 0)
                for s in range(SLICES):
                    gelu(PAIRS - 1, s, lambda j: None)

            @block.vector
            def _(dve):
                LN_LINKS = 17

                def stat_w(src, ws):
                    for w in ws:
                        last = nc.vector.bn_stats(stats[:, w, :], src[:, w * C:(w + 1) * C])
                    return last

                def mean_rstd(i, ln):
                    count = [1]

                    def link(ins):
                        ins.then_inc(ln_step[ln], 1)
                        count[0] += 1
                        return count[0]

                    def need(n):
                        dve.wait_ge(ln_step[ln], i * LN_LINKS + n)

                    need(1)
                    me, ve, mo, vo = (stats[:, :, j] for j in (1, 2, 4, 5))
                    mean, dev, var, rstd, t = (small[:, 5 * ln + j, :] for j in range(5))
                    a = link(nc.vector.tensor_tensor(dev, me, mo, ALU.subtract))
                    link(nc.vector.scalar_tensor_tensor(var, ve, C * EPS_LN, vo, ALU.add, ALU.add))
                    b = link(nc.vector.tensor_tensor(mean, me, mo, ALU.add))
                    need(a)
                    a = link(nc.vector.scalar_tensor_tensor(dev, dev, 0.25, dev, ALU.mult, ALU.mult))
                    need(b)
                    link(nc.vector.tensor_scalar(mean, mean, 0.5, None, ALU.mult))
                    need(a)
                    need(link(nc.vector.scalar_tensor_tensor(var, var, 1.0 / C, dev, ALU.mult, ALU.add)))
                    need(link(nc.vector.tensor_scalar(rstd.bitcast(I32), var.bitcast(I32), -0.5, RSQRT_GUESS, ALU.mult, ALU.add)))
                    for p in range(3):
                        need(link(nc.vector.tensor_tensor(t, rstd, rstd, ALU.mult)))
                        need(link(nc.vector.scalar_tensor_tensor(t, var, -0.5, t, ALU.mult, ALU.mult)))
                        last = nc.vector.scalar_tensor_tensor(rstd, t, 1.5, rstd, ALU.add, ALU.mult)
                        if p < 2:
                            need(link(last))
                    last.then_inc(ln_step[ln], 1)
                    assert count[0] + 1 == LN_LINKS
                    need(LN_LINKS)

                def normalise(src, dst, i, ln, k):
                    w0, n = k * WP, WP
                    mean, rstd = small[:, 5 * ln, w0:w0 + n], small[:, 5 * ln + 3, w0:w0 + n]
                    s = src[:, w0 * C:(w0 + n) * C].rearrange("p (w c) -> p w c", c=C)
                    d = dst[:, w0 * C:(w0 + n) * C].rearrange("p (w c) -> p w c", c=C)
                    nc.vector.tensor_tensor(d, s, bc(mean, n), ALU.subtract).then_inc(norm_step[ln], 1)
                    dve.wait_ge(norm_step[ln], i * 2 + k + 1)
                    return nc.vector.tensor_tensor(d, d, bc(rstd, n), ALU.mult)

                def ln1_stats(i, quarter):
                    dve.wait_ge(a_dve, (i + 1) * 7)
                    n = W // 4
                    last = stat_w(ybuf, range(n * quarter, n * quarter + n))
                    if quarter == 3:
                        last.then_inc(ln_step[0], 1)

                def ln1_norm(i, half):
                    last = normalise(ybuf, h_nat, i, 0, half)
                    if half == 1:
                        last.then_inc(n1_ready, 1)

                def ln2(i, stats_there=False):
                    if not stats_there:
                        dve.wait_ge(b_dve, (i + 1) * B_DVE)
                        stat_w(fbuf, range(W)).then_inc(ln_step[1], 1)
                    mean_rstd(i, 1)
                    for k in range(2):
                        normalise(fbuf, n2, i, 1, k).then_inc(n2_ready, 1)

                def ev_whiten(i, ks):
                    if not isinstance(i, int) or i > 0:
                        dve.wait_ge(r_ready, i)
                    for k in ks:
                        dve.wait_ge(pe_a, i * A_CHUNKS + 7 + k + 1)
                        nc.vector.tensor_tensor(
                            ybuf[:, k * 512:(k + 1) * 512].rearrange("p (w c) -> p w c", c=C),
                            ring_a[(k + 7) % RING_A][0:ROWS, :].rearrange("p (w c) -> p w c", c=C),
                            row("beta", 8), ALU.add).then_inc(a_dve, 1)

                def ev_layer_2(i, half, ks):
                    for k in ks:
                        c = 4 * half + k
                        dve.wait_ge(pe_b, i * B_CHUNKS + L2 + c + 1)
                        if c >= L2_BUFS or not isinstance(i, int) or i > 0:
                            dve.wait_ge(shrunk, i * 8 + c - L2_BUFS + 1)
                        n = L2_KP[k] * 128
                        nc.vector.tensor_tensor(
                            layer2[:, c % L2_BUFS, 0:n].rearrange("p (k m) -> p k m", m=128),
                            ring_b[c % RING_B][0:2 * KR, 0:n].rearrange("p (k m) -> p k m", m=128),
                            pp("fb2", 2 * KR)[:, 128 * half:128 * half + 128].unsqueeze(1).broadcast_to((2 * KR, n // 128, 128)),
                            ALU.add).then_inc(b_dve, 1)

                def ev_rest(i, s):
                    k = 0 if s == 0 else 5 + 6 * (s - 1)
                    dve.wait_ge(pe_c, i * C_CHUNKS + k + 1)
                    for v in range(2):
                        dve.wait_ge(hi_ready, i * 2 * SLICES + 2 * s + v + 1)
                        last = nc.vector.tensor_tensor(n2T[C * (1 - v):C * (1 - v) + C, v, :],
                                                       ring_c[k % RING_C][C * v:C * v + C, 0:4 * ROWS],
                                                       n2T[C * v:C * v + C, v, :].bitcast(F32), ALU.subtract)
                    last.then_inc(c_dve, 1)

                def ev_mlp(i, s):
                    k = 6 + 6 * s if s < SLICES - 1 else C_CHUNKS - 1
                    dve.wait_ge(pe_c, i * C_CHUNKS + k + 1)
                    if s == 0:
                        dve.wait_ge(f_biased, i + 1)
                    uses = 4 if s % 2 == 0 else 3
                    if s >= 2 or not isinstance(i, int) or i > 0:
                        dve.wait_ge(stored[s % 2], 16 * (i * uses + s // 2))
                    nc.vector.tensor_tensor(oslice[:, s % 2, :], ring_c[k % RING_C][0:ROWS, :],
                                            fbuf[:, s * SW * C:(s + 1) * SW * C], ALU.add).then_inc(c_dve, 1)

                def ev_turn(i, ks):
                    for k in ks:
                        dve.wait_ge(pe_b, i * B_CHUNKS + TR + k + 1)
                        turn_copy(nc.vector.tensor_copy, k).then_inc(b_dve, 1)

                def ev_inv_h(i, with_stats=False):
                    dve.wait_ge(r_ready, i + 1)
                    if not isinstance(i, int) or i > 0:
                        dve.wait_ge(c_dve, i * C_DVE)
                    for k in range(8):
                        dve.wait_ge(pe_b, i * B_CHUNKS + FIN + k + 1)
                        nc.vector.tensor_tensor(fbuf[:, k * 7 * C:(k + 1) * 7 * C], ring_b[k % RING_B][0:ROWS, 0:7 * C],
                                                r_nat[:, k * 7 * C:(k + 1) * 7 * C], ALU.add).then_inc(b_dve, 1)
                        if with_stats:
                            dve.wait_ge(b_dve, i * B_DVE + 16 + k + 1)
                            last = stat_w(fbuf, range(7 * k, 7 * k + 7))
                    if with_stats:
                        last.then_inc(ln_step[1], 1)

                def step(i, ahead, behind):
                    def slice_(s, before, after):
                        before()
                        if behind and s < SLICES - 1:
                            ev_rest(i - 1, s + 1)
                        after()
                        if behind:
                            ev_mlp(i - 1, s)

                    def next_(what, *args):
                        if ahead:
                            what(i + 1, *args)

                    if behind:
                        ln2(i - 1)
                        ev_rest(i - 1, 0)
                    slice_(0, lambda: next_(ev_whiten, range(6)), lambda: next_(ev_whiten, [6]))
                    slice_(1, lambda: (ev_layer_2(i, 0, [0, 1, 2]), next_(ln1_stats, 0)),
                           lambda: (ev_layer_2(i, 0, [3]), next_(ln1_stats, 1)))
                    slice_(2, lambda: (ev_layer_2(i, 1, [0, 1, 2]), next_(ln1_stats, 2)),
                           lambda: (ev_layer_2(i, 1, [3]), next_(ln1_stats, 3)))
                    slice_(3, lambda: next_(mean_rstd, 0), lambda: next_(ln1_norm, 0))
                    slice_(4, lambda: next_(ln1_norm, 1), lambda: None)
                    slice_(5, lambda: ev_turn(i, [1, 3, 5]), lambda: ev_turn(i, [7]))
                    slice_(6, lambda: ev_turn(i, [9, 11, 13]), lambda: ev_turn(i, [15]))
                    ev_inv_h(i, with_stats=not ahead)

                ev_whiten(0, range(7))
                for quarter in range(4):
                    ln1_stats(0, quarter)
                mean_rstd(0, 0)
                for half in range(2):
                    ln1_norm(0, half)
                step(0, True, False)
                with dve.Fori(1, PAIRS - 1) as i:
                    step(i, True, True)
                step(PAIRS - 1, False, True)
                ln2(PAIRS - 1, stats_there=True)
                ev_rest(PAIRS - 1, 0)
                for s in range(SLICES):
                    if s < SLICES - 1:
                        ev_rest(PAIRS - 1, s + 1)
                    ev_mlp(PAIRS - 1, s)

            @block.gpsimd
            def _(pool):
                h3, y3, r3, f3 = (t.rearrange("p (w c) -> p w c", c=C) for t in (h_nat, ybuf[:], r_nat, fbuf[:]))

                def scale_h(i):
                    pool.wait_ge(n1_ready, i + 1)
                    nc.gpsimd.tensor_tensor(h3, h3, row("g1", W), ALU.mult).then_inc(h_step, 1)
                    pool.wait_ge(h_step, i + 1)
                    nc.gpsimd.tensor_tensor(h3, h3, row("b1", W), ALU.add).then_inc(h_ready, 1)

                def residual(i):
                    if not isinstance(i, int) or i > 0:
                        pool.wait_ge(b_dve, i * B_DVE)
                    pool.wait_ge(h_ready, i + 1)
                    nc.gpsimd.tensor_tensor(r3, h3, y3, ALU.add).then_inc(r_ready, 1)

                def bias_f(i):
                    pool.wait_ge(n2_ready, 2 * i + 2)
                    nc.gpsimd.tensor_tensor(f3, f3, row("mb2", W), ALU.add).then_inc(f_biased, 1)

                def shrunk_sum(i):
                    for c in range(8):
                        half, k = c // 4, c % 4
                        n = L2_KP[k] * 128
                        pool.wait_ge(shrunk, i * 8 + c + 1)
                        yk = y_v[0:2 * KR, 4 * k:4 * k + L2_KP[k], :].rearrange("p k (m h j) -> p h k m j", h=2, j=CH)[:, half]
                        a, b = (m[:, c % L2_BUFS, 0:n].rearrange("p (k m j) -> p k m j", m=4, j=CH) for m in (over, under))
                        nc.gpsimd.tensor_tensor(yk, a, b, ALU.subtract).then_inc(y_ready, 1)

                scale_h(0)
                residual(0)
                shrunk_sum(0)
                scale_h(1)
                with pool.Fori(1, PAIRS - 1) as i:
                    residual(i)
                    bias_f(i - 1)
                    shrunk_sum(i)
                    scale_h(i + 1)
                residual(PAIRS - 1)
                bias_f(PAIRS - 2)
                shrunk_sum(PAIRS - 1)
                bias_f(PAIRS - 1)


GR = C + KR
TURN_M = 65
L2_KP = [4, 4, 4, KHP - 12]
L2_BUFS = 2
L1_PARTS = [(0, 15), (15, KF)]
TURN_W = [(7 * (k // 2) + (0 if k % 2 == 0 else 4), 4 if k % 2 == 0 else 3) for k in range(16)]


def constants():
    at, n = offsets(CONST_COLS)
    c = np.zeros((128, n), np.float32)

    def put(name, m):
        c[:m.shape[0], at[name][0]:at[name][1]] = m.reshape(m.shape[0], -1)

    pos, k = np.arange(H), np.arange(KF)
    cos = np.cos(2 * np.pi * (np.outer(pos, k) % H) / H)
    sin = np.sin(2 * np.pi * (np.outer(pos, k) % H) / H)
    f1 = np.zeros((2, H, KF, 2, 2))
    for b in range(2):
        f1[b, :, :, b, 0] = cos / H
        f1[b, :, :, b, 1] = -sin / H
    put("f1", f1.reshape(ROWS, -1))
    f2 = np.zeros((W, 2, 2, 2, KF))
    for h in range(2):
        f2[:, h, 0, h, :] = cos
        f2[:, h, 1, h, :] = sin
    put("f2", f2.reshape(ROWS, -1))
    wk = np.where((k == 0) | (k == KF - 1), 0.5, 1.0)
    inv = np.zeros((2, 2, KF, 2, 2, 2, W))
    for q in range(2):
        for s, sign in enumerate((1.0, -1.0)):
            inv[q, s, :, 0, q, 0] = (wk * cos).T
            inv[q, s, :, 0, q, 1] = sign * (wk * sin).T
            inv[q, s, :, 1, q, 0] = -(wk * sin).T
            inv[q, s, :, 1, q, 1] = sign * (wk * cos).T
    put("invw", inv.reshape(2 * KR, -1))
    ih = np.zeros((2, 64, 2, H))
    for b in range(2):
        ih[b, 0:KR:2, b] = (2 * wk * cos).T / H
        ih[b, 1:KR:2, b] = -(2 * wk * sin).T / H
    put("invh", ih.reshape(128, -1))
    same = np.kron(np.eye(CH // BS), np.ones((BS, BS)))
    m1 = np.zeros((2, 2, CH, 2, 2, CH))
    for cs, r in ((0, 0), (0, 1), (1, 0), (1, 1)):
        for s, sign in enumerate((1.0, -1.0)):
            to_re = (cs == r)
            coef = {(0, 0): 1.0, (1, 1): sign, (0, 1): sign, (1, 0): -1.0}[cs, r]
            m1[cs, r, :, s, 0] = same * coef * (1.0 if to_re else -1.0)
            m1[cs, r, :, s, 1] = same * coef
    put("mask1", m1.reshape(128, -1))
    m2 = np.zeros((2, 2, CH, 2, 2, CH))
    for b in range(2):
        for r in range(2):
            m2[b, r, :, 0, b] = same * (1.0 if r == 0 else -1.0)
            m2[b, r, :, 1, b] = same
    put("mask2", m2.reshape(128, -1))
    put("below", -np.tril(np.ones((C, C)), -1))
    put("ident", np.eye(128))
    put("pilot", np.full((ROWS, 128), 1.0 / ROWS))
    return c


def layout(i):
    at, n = offsets(PARAM_COLS)
    p = np.zeros((128, n), np.float32)

    def put(name, m):
        p[:m.shape[0], at[name][0]:at[name][1]] = m.reshape(m.shape[0], -1)

    def rows(v):
        return np.broadcast_to(v.reshape(1, -1), (128, v.size))

    G = CH // BS
    w1 = i["L1_conv_w1"].reshape(2, 2, G, BS, BS)
    w2 = i["L1_conv_w2"].reshape(2, 2, G, BS, BS)
    a = np.zeros((2, 2, G, BS, 2, 2, 2, G, BS), np.float32)
    for cs in range(2):
        for r in range(2):
            for ro in range(2):
                part = ro if cs == r else 1 - ro
                a[cs, r, :, :, :, :, ro] = w1[part].transpose(1, 2, 0, 3)[:, :, :, None, None, :]
    put("w1", a.reshape(128, -1))
    a = np.zeros((2, 2, G, BS, 2, 2, 2, G, BS), np.float32)
    for r in range(2):
        for ro in range(2):
            part = ro if r == 0 else 1 - ro
            a[:, r, :, :, :, ro] = w2[part].transpose(1, 2, 0, 3)[None, :, :, :, None, None, :]
    put("w2", a.reshape(128, -1))
    put("mw1", np.tile(i["L1_conv_mw1"], (2, 1)))
    m = np.zeros((HH, 2, 128), np.float32)
    m[:, :, 32:32 + C] = i["L1_conv_mw2"].reshape(2, HH, C).transpose(1, 0, 2)
    put("mw2", m)
    put("beta", rows(i["L0_conv_beta"]))
    put("g1", rows(i["L1_conv_n1_g"]))
    put("b1", rows(i["L1_conv_n1_b"]))
    put("mb2", rows(i["L1_conv_mb2"]))
    fb2 = i["L1_conv_b2"].reshape(2, 2, CH).transpose(1, 0, 2)
    put("fb2", rows(np.broadcast_to(fb2[:, :, None, :], (2, 2, 2, CH))))
    put("gamma", i["L0_conv_gamma"].reshape(C, 1))
    put("g2", np.tile(i["L1_conv_n2_g"], 2).reshape(128, 1))
    put("b2", np.tile(i["L1_conv_n2_b"], 2).reshape(128, 1))
    fb1 = i["L1_conv_b1"].reshape(2, 2, CH).transpose(0, 2, 1)
    put("fb1", np.broadcast_to(fb1[None], (2, 2, CH, 2)).reshape(128, 2))
    put("mb1", i["L1_conv_mb1"].reshape(2, HH).T)
    return p


def kernel(**inputs):
    import numpy as _np
    import concourse.bacc as _bacc
    from concourse.bass_utils import run_bass_kernel_spmd as _run

    i = {k: _np.asarray(v) for k, v in inputs.items()}
    arrays = {"x_dram": _np.ascontiguousarray(i["x"]), "consts_dram": constants(), "params_dram": layout(i)}
    nc = _bacc.Bacc("TRN2", target_bir_lowering=False, num_devices=1)
    aps = {k: nc.dram_tensor(k, v.shape, F32, kind="ExternalInput").ap() for k, v in arrays.items()}
    out = nc.dram_tensor("out_dram", (B, H, W, C), F32, kind="ExternalOutput").ap()
    build(nc, aps["x_dram"], aps["consts_dram"], aps["params_dram"], out)
    r = _run(nc, [arrays], core_ids=[0])
    return r.results[0]["out_dram"]
```

```python
from contextlib import ExitStack

import numpy as np

import concourse.bass as bass
from concourse import mybir

F32 = mybir.dt.float32
F32R = mybir.dt.float32r
I32 = mybir.dt.int32
ALU = mybir.AluOpType
ACT = mybir.ActivationFunctionType
AX_X = mybir.AxisListType.X

B, H, W, C = 16, 56, 56, 64
N_TOK = B * H * W
NB = 8
BS = C // NB
HID = 4 * C
KF = H // 2 + 1
PAIRS = B // 2
ROWS = 2 * H
FREE = W * C
WP = W // 2
CH = C // 2
KR = 2 * KF
KHP = (KF + 1) // 2
SPEC = KF * KF
EPS_COV, EPS_LN, LAM = 1e-3, 1e-5, 0.01
HH = HID // 2
RSQRT_GUESS = 1597463007.0
SLICES = 7
SW = W // SLICES

S1, S2, L1, L2, INVW, TR, B_CHUNKS = 0, 8, 16, 24, 32, 40, 56
A_CHUNKS, C_CHUNKS = 14, 42
RING_A, RING_B, RING_C = 2, 4, 2
C_ACT, C_DVE = 28, 14

GR = C + KR
L2_KP = [4, 4, 4, KHP - 12]
L2_BUFS = 2
MEMSETS = 7
L1_PARTS = [(0, 15), (15, KF)]
TURN_WP = [(7 * (k // 2) + (0 if k % 2 == 0 else 4), 4 if k % 2 == 0 else 3) for k in range(8)]


def first(i):
    return isinstance(i, int) and i == 0


def last_pair(i):
    return isinstance(i, int) and i == PAIRS - 1


def tr_at(k):
    return TR + k if k < 4 else TR + 4 + 2 * (k - 4)


def fin_at(k):
    return TR + 5 + 2 * k if k < 4 else TR + 8 + k


L1_DVE = (4, 6)
B_READERS = [("act",)] * B_CHUNKS
for _k in range(8):
    B_READERS[L2 + _k] = ("dve",)
    B_READERS[tr_at(_k)] = ("act", "dve")
    B_READERS[fin_at(_k)] = ("dve",)
for _k in L1_DVE:
    B_READERS[L1 + _k] = ("dve",)


def b_done(who, k):
    return sum(who in readers for readers in B_READERS[:k + 1])


B_ACT, B_DVE = (b_done(who, B_CHUNKS - 1) for who in ("act", "dve"))


X_BESIDE = {1: [[0], [], [1], []], 2: [[2], [], [3], []], 3: [[4], [5], [6], []]}


def lo_done(s):
    return 1 if s == 0 else 2 * s


def out_done(s):
    return C_DVE if s == SLICES - 1 else 2 * s + 3


def c_reader(k):
    if k == 0:
        return "dve", lo_done(0)
    s, j = (k - 1) // 6, (k - 1) % 6
    if j < 4:
        return "act", 4 * s + j + 1
    if j == 4 and s < SLICES - 1:
        return "dve", lo_done(s + 1)
    return "dve", out_done(s)


CONST_COLS = {"f1": 2 * KR, "f2": 4 * KF, "invw": 2 * 224, "invh": ROWS, "mask1": 128, "mask2": 128,
              "below": C, "minus": C, "ident": 128}
PARAM_COLS = {"w1": 256, "w2": 256, "mw1": HID, "mw2": 2 * 128, "beta": C, "g1": C, "b1": C, "mb2": C,
              "fb2": 256, "gamma": 1, "g2": 1, "b2": 1, "fb1": 2, "mb1": 2}


def offsets(cols):
    at, out = 0, {}
    for name, n in cols.items():
        out[name] = (at, at + n)
        at += n
    return out, at


def build(nc, x, consts, params, out):
    c_at, c_n = offsets(CONST_COLS)
    p_at, p_n = offsets(PARAM_COLS)
    x_v = x.rearrange("(t b) h w c -> t (b h) (w c)", b=2)
    out_v = out.rearrange("(t b) h w c -> t (b h) (w c)", b=2)

    with ExitStack() as ctx:
        def sb(name, shape, dtype=F32):
            return ctx.enter_context(nc.sbuf_tensor(name, shape, dtype))

        def sem(name):
            return ctx.enter_context(nc.semaphore(name))

        cst = sb("cst", [128, c_n])
        prm = sb("prm", [128, p_n])

        def cc(name, rows=128):
            return cst[0:rows, c_at[name][0]:c_at[name][1]]

        def pp(name, rows=128):
            return prm[0:rows, p_at[name][0]:p_at[name][1]]

        ident = cc("ident")
        wy = sb("wy", [128, 128])
        w1s = sb("w1s", [128, 256])
        w2s = sb("w2s", [128, 256])
        mw1s = sb("mw1s", [128, HID])
        mw1h = sb("mw1h", [128, HID], F32R)
        mw1l = sb("mw1l", [128, HID], F32R)
        hbias = sb("hbias", [128, 2])
        negm = sb("negm", [128, 1])

        CW = 130
        xin = sb("xin", [ROWS, FREE])
        ybuf = sb("ybuf", [ROWS, FREE])
        hbuf = sb("hbuf", [ROWS, WP * CW])
        rbuf = sb("rbuf", [ROWS, WP * CW])
        fbuf = sb("fbuf", [ROWS, FREE])
        n2 = sb("n2", [ROWS, FREE])
        xT = sb("xT", [128, WP * ROWS])
        u_r = sb("u_r", [128, CH * 2 * KR])
        p_y = sb("p_y", [128, KHP * 256])
        o_g = sb("o_g", [128, FREE])
        n2T = sb("n2T", [128, 2, 4 * ROWS], F32R)
        hid = sb("hid", [HH, 2, 2, 4 * ROWS])
        oslice = sb("oslice", [ROWS, 2, SW * C])
        layer2 = sb("layer2", [2 * KR, L2_BUFS, 512])
        over = sb("over", [2 * KR, L2_BUFS, 512])
        under = sb("under", [2 * KR, L2_BUFS, 512])
        neg_lam = sb("neg_lam", [128, 1])
        stats = sb("stats", [ROWS, W, 6])
        small = sb("small", [ROWS, 10, W])

        psum = ctx.enter_context(nc.psum_tensor("psum", [128, 8, 512], F32))

        s_cst, s_prm, s_x = sem("s_cst"), sem("s_prm"), [sem(f"s_x{j}") for j in range(4)]
        s_ones, s_pilot, s_pilot_sb = sem("s_ones"), sem("s_pilot"), sem("s_pilot_sb")
        s_cent, s_gram = sem("s_cent"), sem("s_gram")
        s_first, s_cent_part = [sem(f"s_first{q}") for q in range(4)], sem("s_cent_part")
        s_dve, s_pe = sem("s_dve"), sem("s_pe")

        gram = psum[:, 0, 0:CW]
        pil = psum[:, 1, 0:C]
        row_ps = psum[0:1, 2, 0:C]
        outer_ps = psum[0:C, 3, 0:C]
        mcol_ps = psum[:, 4, 0:1]
        rowk_ps = [psum[0:C, 5 + j, 0:C + 1] for j in range(2)]
        wt_ps = psum[0:C, 7, 0:C]
        hb_ps = psum[:, 4, 8:10]
        pilot = sb("pilot", [128, C])
        pilot_w = sb("pilot_w", [ROWS, 128])
        gtmp = sb("gtmp", [C, C + 2])
        elim = sb("elim", [C, 2, 2 * C])
        ahead_v = sb("ahead_v", [C, 2])
        pivot_inv = sb("pivot_inv", [C, 2])
        mult = sb("mult", [C, 2])
        rowd = sb("rowd", [1, 4 * C])
        scol = sb("scol", [C, 4])
        ediag = sb("ediag", [C, C])

        DV_WEIGHTS = 7
        DV_MEAN = DV_WEIGHTS + 11
        DV_COV = DV_MEAN + 1
        DV_DIAG = DV_COV + 4 * (C - 1) - 1 + 3
        DV_W = DV_DIAG + 1 + 3 * 3 + 2
        DV_WY = DV_W + 2
        DV_ALL = DV_WY + 1
        PE_MEAN, PE_HB = 3, 4

        xbuf = [xin, ybuf, fbuf, n2]
        cent = [hbuf, rbuf]

        x_in, pe_a, pe_b, pe_c = sem("x_in"), sem("pe_a"), sem("pe_b"), sem("pe_c")
        a_act, a_dve = sem("a_act"), sem("a_dve")
        b_act, b_dve = sem("b_act"), sem("b_dve")
        c_act, c_dve = sem("c_act"), sem("c_dve")
        ln_step = [sem("ln1_step"), sem("ln2_step")]
        norm_step = [sem("norm1_step"), sem("norm2_step")]
        h0_step, h0_half = sem("h0_step"), sem("h0_half")
        shrunk, y_ready = sem("shrunk"), sem("y_ready")
        n1_ready, h_ready, r_ready = sem("n1_ready"), sem("h_ready"), sem("r_ready")
        n2_ready, f_biased, hi_ready = sem("n2_ready"), sem("f_biased"), sem("hi_ready")
        stored = [sem("stored0"), sem("stored1")]

        ring_a = [psum[:, j, :] for j in range(RING_A)]
        ring_b = [psum[:, RING_A + j, :] for j in range(RING_B)]
        ring_c = [psum[:, RING_A + RING_B + j, :] for j in range(RING_C)]

        u_v = u_r[0:ROWS, :].rearrange("p (m j) -> p m j", j=CH)
        r_v = u_r[:, 0:W * 64].rearrange("p (w m) -> p w m", m=64)
        p_v = p_y[:, 0:2 * 2 * SPEC].rearrange("p (b h k w) -> p b h k w", b=2, h=2, k=KF)
        o_v = o_g[:, 0:2 * 2 * SPEC].rearrange("p (h k s w) -> p h s k w", h=2, s=2, k=KF)
        y_v = p_y[:].rearrange("p (k m) -> p k m", m=256)
        h_nat = hbuf[:, 0:FREE]
        r_nat = rbuf[:, 0:FREE]
        h_w = h_nat.rearrange("p (m j) -> p m j", j=CH)

        def quarter(q, cols):
            return slice(q * WP // 4 * cols, (q + 1) * WP // 4 * cols)

        def bc(ap2, n):
            return ap2.unsqueeze(2).broadcast_to((ROWS, n, C))

        def row(name, n):
            return pp(name, ROWS).unsqueeze(1).broadcast_to((ROWS, n, C))

        def layer_1_parts(k):
            part, half, b = k // 4, k // 2 % 2, k % 2
            a, z = L1_PARTS[part]
            t = ring_b[k % RING_B][:, 0:(z - a) * KF]
            return [(o_v[C * b:C * b + C, half, s, a:z, :], t[C * s:C * s + C, :].rearrange("p (k w) -> p k w", w=KF),
                     pp("fb1")[C * s:C * s + C, half:half + 1]) for s in range(2)]

        def turn_copy(copy, v, k):
            w0, n = TURN_WP[k]
            t = ring_b[tr_at(k) % RING_B][64 * v:64 * v + KR, 0:n * 128].rearrange("p (w b c) -> p b w c", b=2, c=C)
            g = o_g[:].rearrange("p (w v c) -> p w v c", v=2, c=C)
            for b in range(2):
                last = copy(g[C * b:C * b + KR, w0:w0 + n, v, :], t[:, b])
            return last

        with nc.Block() as block:

            @block.sync
            def _(sp):
                def load_for_covariance():
                    for q in range(4):
                        sp.dma_start(xin[:, quarter(q, 2 * C)], x_v[0][:, quarter(q, 2 * C)]).then_inc(s_first[q], 16)
                    for t in range(1, PAIRS):
                        if t >= 4:
                            sp.wait_ge(s_cent, t - 3)
                        sp.dma_start(xbuf[t % 4][:], x_v[t]).then_inc(s_x[t % 4], 16)
                        if t == 2:
                            sp.dma_start(cst[:], consts).then_inc(s_cst, 16)
                        if t == 3:
                            sp.dma_start(prm[:], params).then_inc(s_prm, 16)

                def load(p):
                    src = x_v[p] if isinstance(p, int) else x_v[bass.ds(p, 1)].rearrange("o p f -> (o p) f")
                    sp.dma_start(xin[:], src).then_inc(x_in, 16)

                def store(p, s):
                    sp.wait_ge(c_dve, p * C_DVE + out_done(s))
                    o = out_v[p] if isinstance(p, int) else out_v[bass.ds(p, 1)].rearrange("o p f -> (o p) f")
                    sp.dma_start(o[:, s * SW * C:(s + 1) * SW * C], oslice[:, s % 2, :]).then_inc(stored[s % 2], 16)

                load_for_covariance()
                sp.wait_ge(s_cent, PAIRS - 3)
                load(0)
                sp.wait_ge(pe_a, 7)
                load(1)
                sp.wait_ge(pe_a, A_CHUNKS + 7)
                load(2)
                with sp.Fori(1, PAIRS - 2) as i:
                    sp.wait_ge(pe_a, (i + 1) * A_CHUNKS + 7)
                    load(i + 2)
                    for s in range(SLICES):
                        store(i - 1, s)
                for p in range(PAIRS - 3, PAIRS):
                    for s in range(SLICES):
                        store(p, s)
                sp.wait_ge(stored[0], 16 * 4 * PAIRS)
                sp.wait_ge(stored[1], 16 * 3 * PAIRS)

            @block.gpsimd
            def _(pool):
                nc.gpsimd.memset(pilot_w[:], 1.0 / ROWS).then_inc(s_ones, 1)
                for t in cent:
                    nc.gpsimd.memset(t[:].rearrange("p (w k) -> p w k", k=CW)[:, :, 2 * C:CW], 1.0).then_inc(s_ones, 1)
                nc.gpsimd.memset(neg_lam[:], -LAM).then_inc(s_ones, 1)
                nc.gpsimd.memset(wy[:], 0.0).then_inc(s_ones, 1)
                nc.gpsimd.memset(o_g[:], 0.0).then_inc(s_ones, 1)
                nc.gpsimd.memset(u_r[:], 0.0).then_inc(s_ones, 1)

                h3, y3, r3, f3 = (t.rearrange("p (w c) -> p w c", c=C) for t in (h_nat, ybuf[:], r_nat, fbuf[:]))

                def bias_h(i):
                    for k in range(1 if first(i) else 2):
                        h = h3[:, k * WP:(k + 1) * WP]
                        pool.wait_ge(n1_ready, i * 2 + k + (1 if first(i) else 0))
                        nc.gpsimd.tensor_tensor(h, h, row("b1", WP), ALU.add).then_inc(h_ready, 1)

                def residual(i):
                    if not first(i):
                        pool.wait_ge(b_dve, i * B_DVE)
                    pool.wait_ge(h_ready, i * 2 + 1)
                    nc.gpsimd.tensor_tensor(r3, h3, y3, ALU.add).then_inc(r_ready, 1)

                def bias_f(i):
                    if last_pair(i):
                        for k in range(2):
                            pool.wait_ge(n2_ready, 2 * i + k + 1)
                            f = f3[:, k * WP:(k + 1) * WP]
                            nc.gpsimd.tensor_tensor(f, f, row("mb2", WP), ALU.add).then_inc(f_biased, 1)
                    else:
                        pool.wait_ge(n2_ready, 2 * i + 2)
                        nc.gpsimd.tensor_tensor(f3, f3, row("mb2", W), ALU.add).then_inc(f_biased, 1)

                def shrunk_sum(i):
                    for c in range(8):
                        half, k = c // 4, c % 4
                        n = L2_KP[k] * 128
                        pool.wait_ge(shrunk, i * 8 + c + 1)
                        yk = y_v[0:2 * KR, 4 * k:4 * k + L2_KP[k], :].rearrange("p k (m h j) -> p h k m j", h=2, j=CH)[:, half]
                        a, b = (m[:, c % L2_BUFS, 0:n].rearrange("p (k m j) -> p k m j", m=4, j=CH) for m in (over, under))
                        nc.gpsimd.tensor_tensor(yk, a, b, ALU.subtract).then_inc(y_ready, 1)

                pool.wait_ge(s_prm, 16)
                bias_h(0)
                pool.wait_ge(h0_half, 1)
                residual(0)
                shrunk_sum(0)
                bias_h(1)
                with pool.Fori(1, PAIRS - 1) as i:
                    residual(i)
                    bias_f(i - 1)
                    shrunk_sum(i)
                    bias_h(i + 1)
                residual(PAIRS - 1)
                bias_f(PAIRS - 2)
                shrunk_sum(PAIRS - 1)
                bias_f(PAIRS - 1)

            @block.vector
            def _(dve):
                def rsqrt_newton(r, v, t, link):
                    link(nc.vector.tensor_scalar(r.bitcast(I32), v.bitcast(I32), -0.5, RSQRT_GUESS, ALU.mult, ALU.add))
                    for _ in range(3):
                        link(nc.vector.tensor_tensor(t, r, r, ALU.mult))
                        link(nc.vector.scalar_tensor_tensor(t, v, -0.5, t, ALU.mult, ALU.mult))
                        link(nc.vector.scalar_tensor_tensor(r, t, 1.5, r, ALU.add, ALU.mult))

                def covariance_and_factor():
                    count = [0]

                    def link(ins, wait=True):
                        ins.then_inc(s_dve, 1)
                        count[0] += 1
                        if wait:
                            dve.wait_ge(s_dve, count[0])

                    dve.wait_ge(s_pilot, 1)
                    nc.vector.tensor_copy(pilot[:], pil).then_inc(s_pilot_sb, 1)
                    dve.wait_ge(s_pilot_sb, 1)
                    dve.wait_ge(s_ones, 3)

                    def centred(t, cols_out, cols_in):
                        n = (cols_in.stop - cols_in.start) // (2 * C)
                        return nc.vector.tensor_tensor(
                            cent[t % 2][:, cols_out].rearrange("p (w k) -> p w k", k=CW)[:, :, 0:2 * C].rearrange("p w (t c) -> p w t c", t=2),
                            xbuf[t % 4][:, cols_in].rearrange("p (w t c) -> p w t c", t=2, c=C),
                            pilot[0:ROWS, :].unsqueeze(1).unsqueeze(1).broadcast_to((ROWS, n, 2, C)),
                            ALU.subtract)

                    def centre(t):
                        dve.wait_ge(s_x[t % 4], 16 * (t // 4) + (0 if t % 4 == 0 else 16))
                        if t >= 2:
                            dve.wait_ge(s_gram, t - 1)
                        centred(t, slice(0, WP * CW), slice(0, FREE)).then_inc(s_cent, 1)

                    for q in range(4):
                        if q > 0:
                            dve.wait_ge(s_first[q], 16)
                        centred(0, quarter(q, CW), quarter(q, 2 * C)).then_inc(s_cent_part if q < 3 else s_cent, 1)
                    for t in range(1, PAIRS):
                        centre(t)

                    dve.wait_ge(s_cst, 16)
                    dve.wait_ge(s_prm, 16)
                    for t, src, mask in ((w1s, "w1", "mask1"), (w2s, "w2", "mask2")):
                        for h in range(2):
                            link(nc.vector.tensor_tensor(t[:, 128 * h:128 * h + 128],
                                                         pp(src)[:, 128 * h:128 * h + 128], cc(mask), ALU.mult))
                    link(nc.vector.tensor_scalar(mw1s[:], pp("mw1"), pp("g2"), None, ALU.mult))
                    link(nc.vector.tensor_copy(mw1h[:], mw1s[:]))
                    link(nc.vector.tensor_tensor(mw1l[:], mw1s[:], mw1h[:].bitcast(F32), ALU.subtract))
                    assert count[0] == DV_WEIGHTS

                    dve.wait_ge(s_gram, PAIRS)
                    link(nc.vector.tensor_copy(gtmp[:], gram[C:2 * C, C:CW]))
                    link(nc.vector.tensor_tensor(gtmp[:, 0:C], gram[0:C, 0:C], gtmp[:, 0:C], ALU.add))
                    link(nc.vector.tensor_tensor(gtmp[:, C:C + 1], gram[0:C, 2 * C:2 * C + 1], gtmp[:, C:C + 1], ALU.add))
                    dve.wait_ge(s_pe, 1)
                    link(nc.vector.tensor_scalar(rowd[:, 0:C], row_ps, 1.0 / N_TOK, None, ALU.mult))
                    link(nc.vector.scalar_tensor_tensor(
                        rowd[:, 2 * C:3 * C], pilot[0:1, :], -1.0, rowd[:, 0:C], ALU.mult, ALU.subtract))
                    link(nc.vector.tensor_copy(rowd[:, 3 * C:4 * C], rowd[:, 2 * C:3 * C]))
                    dve.wait_ge(s_pe, 2)
                    link(nc.vector.scalar_tensor_tensor(
                        gtmp[:, 0:C], outer_ps, -float(N_TOK), gtmp[:, 0:C], ALU.mult, ALU.add))
                    link(nc.vector.tensor_scalar(
                        gtmp[:, 0:C], gtmp[:, 0:C], 1.0 / (N_TOK - 1.0), 1.0 - EPS_COV, ALU.mult, ALU.mult))
                    link(nc.vector.tensor_copy(elim[:, 0, C:2 * C], ident[0:C, 0:C]))
                    link(nc.vector.tensor_copy(elim[:, 1, C:2 * C], ident[0:C, 0:C]))
                    dve.wait_ge(s_pe, PE_MEAN)
                    link(nc.vector.tensor_copy(negm[:], mcol_ps))
                    assert count[0] == DV_MEAN
                    link(nc.vector.scalar_tensor_tensor(
                        elim[:, 0, 0:C], ident[0:C, 0:C], EPS_COV, gtmp[:, 0:C], ALU.mult, ALU.add))
                    assert count[0] == DV_COV
                    for k in range(C - 1):
                        now, row_k = elim[:, k % 2, :], rowk_ps[k % 2]
                        dve.wait_ge(s_pe, PE_HB + k + 1)
                        inv = pivot_inv[:, k % 2:k % 2 + 1]
                        link(nc.vector.reciprocal(inv, row_k[:, 0:1]))
                        if k < C - 2:
                            link(nc.vector.scalar_tensor_tensor(
                                ahead_v[:, k % 2:k % 2 + 1], row_k[:, 1:2], inv, cc("minus", C)[:, k:k + 1],
                                ALU.mult, ALU.mult), wait=False)
                        link(nc.vector.scalar_tensor_tensor(
                            mult[:, k % 2:k % 2 + 1], now[:, k:k + 1], inv, cc("below", C)[:, k:k + 1],
                            ALU.mult, ALU.mult))
                        link(nc.vector.scalar_tensor_tensor(
                            elim[:, (k + 1) % 2, k + 1:k + 1 + C], row_k[:, 1:C + 1], mult[:, k % 2:k % 2 + 1],
                            now[:, k + 1:k + 1 + C], ALU.mult, ALU.add), wait=False)
                    dve.wait_ge(s_dve, count[0])
                    for j in range(2):
                        link(nc.vector.tensor_tensor(ediag[:, j::2], elim[:, j, j:C:2], ident[0:C, j:C:2], ALU.mult))
                    link(nc.vector.reduce_sum(scol[:, 1:2], ediag[:], AX_X))
                    assert count[0] == DV_DIAG
                    rsqrt_newton(scol[:, 2:3], scol[:, 1:2], scol[:, 0:1], link)
                    link(nc.vector.tensor_tensor(scol[:, 3:4], scol[:, 2:3], pp("gamma", C), ALU.mult))
                    link(nc.vector.tensor_scalar(ediag[:], elim[:, (C - 1) % 2, C:2 * C], scol[:, 3:4], None, ALU.mult))
                    assert count[0] == DV_W
                    dve.wait_ge(s_pe, PE_HB + C - 1 + 1)
                    dve.wait_ge(s_ones, MEMSETS)
                    link(nc.vector.tensor_copy(wy[0:C, 0:C], wt_ps))
                    link(nc.vector.tensor_copy(wy[C:2 * C, C:2 * C], wt_ps))
                    assert count[0] == DV_WY
                    dve.wait_ge(s_pe, PE_HB)
                    link(nc.vector.tensor_tensor(hbias[:], hb_ps, pp("mb1"), ALU.add))
                    assert count[0] == DV_ALL

                LN_LINKS = 17

                def stat_w(src, ws):
                    for w in ws:
                        last = nc.vector.bn_stats(stats[:, w, :], src[:, w * C:(w + 1) * C])
                    return last

                def mean_rstd(i, ln, half=None):
                    count = [1]
                    ws = slice(0, W) if half is None else slice(WP * half, WP * half + WP)

                    def link(ins):
                        ins.then_inc(ln_step[ln], 1)
                        count[0] += 1
                        return count[0]

                    def need(n):
                        dve.wait_ge(ln_step[ln], i * LN_LINKS + n + (LN_LINKS if half == 1 else 0))

                    need(1)
                    me, ve, mo, vo = (stats[:, ws, j] for j in (1, 2, 4, 5))
                    mean, dev, var, rstd, t = (small[:, 5 * ln + j, ws] for j in range(5))
                    a = link(nc.vector.tensor_tensor(dev, me, mo, ALU.subtract))
                    link(nc.vector.scalar_tensor_tensor(var, ve, C * EPS_LN, vo, ALU.add, ALU.add))
                    b = link(nc.vector.tensor_tensor(mean, me, mo, ALU.add))
                    need(a)
                    a = link(nc.vector.scalar_tensor_tensor(dev, dev, 0.25, dev, ALU.mult, ALU.mult))
                    need(b)
                    link(nc.vector.tensor_scalar(mean, mean, 0.5, None, ALU.mult))
                    need(a)
                    need(link(nc.vector.scalar_tensor_tensor(var, var, 1.0 / C, dev, ALU.mult, ALU.add)))
                    rsqrt_newton(rstd, var, t, lambda ins: need(link(ins)))
                    assert count[0] == LN_LINKS

                def norm_count(i, ln, n):
                    return i * (4 if ln == 0 else 2) + n

                def half_w(t, k):
                    return t[:, k * WP * C:(k + 1) * WP * C].rearrange("p (w c) -> p w c", c=C)

                def subtract_mean(src, dst, ln, k):
                    nc.vector.tensor_tensor(half_w(dst, k), half_w(src, k), bc(small[:, 5 * ln, k * WP:(k + 1) * WP], WP),
                                            ALU.subtract).then_inc(norm_step[ln], 1)

                def multiply_rstd(dst, i, ln, k):
                    dve.wait_ge(norm_step[ln], norm_count(i, ln, 2 * k + 1 if ln == 0 else k + 1))
                    return nc.vector.tensor_tensor(half_w(dst, k), half_w(dst, k),
                                                   bc(small[:, 5 * ln + 3, k * WP:(k + 1) * WP], WP), ALU.mult)

                def ln1_stats(i, parts):
                    dve.wait_ge(a_dve, (i + 1) * 7)
                    for q in parts:
                        last = stat_w(ybuf, range(7 * q, 7 * q + 7))
                        if q == 7:
                            last.then_inc(ln_step[0], 1)

                def ln1_subtract(i, k):
                    subtract_mean(ybuf, h_nat, 0, k)

                def ln1_rstd(i, k):
                    multiply_rstd(h_nat, i, 0, k).then_inc(norm_step[0], 1)

                def ln1_gain(i, k):
                    dve.wait_ge(norm_step[0], norm_count(i, 0, 2 * k + 2))
                    return nc.vector.tensor_tensor(half_w(h_nat, k), half_w(h_nat, k), row("g1", WP), ALU.mult)

                def ln1_last(i, k):
                    ln1_gain(i, k).then_inc(n1_ready, 1)

                def ln2(i):
                    mean_rstd(i, 1)
                    for k in range(2):
                        subtract_mean(fbuf, n2, 1, k)
                        multiply_rstd(n2, i, 1, k).then_inc(n2_ready, 1)

                def ev_whiten(i, ks):
                    if not first(i):
                        dve.wait_ge(r_ready, i)
                    for k in ks:
                        dve.wait_ge(pe_a, i * A_CHUNKS + 7 + k + 1)
                        nc.vector.tensor_tensor(
                            ybuf[:, k * 512:(k + 1) * 512].rearrange("p (w c) -> p w c", c=C),
                            ring_a[(k + 7) % RING_A][0:ROWS, :].rearrange("p (w c) -> p w c", c=C),
                            row("beta", 8), ALU.add).then_inc(a_dve, 1)

                def ev_layer_1(i):
                    for k in L1_DVE:
                        dve.wait_ge(pe_b, i * B_CHUNKS + L1 + k + 1)
                        for dst, src, bias in layer_1_parts(k):
                            last = nc.vector.tensor_scalar(dst, src, bias, 0.0, ALU.add, ALU.max)
                        last.then_inc(b_dve, 1)

                def ev_layer_2(i, half, ks):
                    for k in ks:
                        c = 4 * half + k
                        dve.wait_ge(pe_b, i * B_CHUNKS + L2 + c + 1)
                        if c >= L2_BUFS or not first(i):
                            dve.wait_ge(shrunk, i * 8 + c - L2_BUFS + 1)
                        n = L2_KP[k] * 128
                        nc.vector.tensor_tensor(
                            layer2[:, c % L2_BUFS, 0:n].rearrange("p (k m) -> p k m", m=128),
                            ring_b[c % RING_B][0:2 * KR, 0:n].rearrange("p (k m) -> p k m", m=128),
                            pp("fb2", 2 * KR)[:, 128 * half:128 * half + 128].unsqueeze(1).broadcast_to((2 * KR, n // 128, 128)),
                            ALU.add).then_inc(b_dve, 1)

                def ev_rest(i, s):
                    k = 0 if s == 0 else 5 + 6 * (s - 1)
                    dve.wait_ge(pe_c, i * C_CHUNKS + k + 1)
                    for v in range(2):
                        dve.wait_ge(hi_ready, i * 2 * SLICES + 2 * s + v + 1)
                        last = nc.vector.tensor_tensor(n2T[C * (1 - v):C * (1 - v) + C, v, :],
                                                       ring_c[k % RING_C][C * v:C * v + C, 0:4 * ROWS],
                                                       n2T[C * v:C * v + C, v, :].bitcast(F32), ALU.subtract)
                    last.then_inc(c_dve, 1)

                def ev_mlp(i, s):
                    k = 6 + 6 * s if s < SLICES - 1 else C_CHUNKS - 1
                    dve.wait_ge(pe_c, i * C_CHUNKS + k + 1)
                    if s == 0:
                        dve.wait_ge(f_biased, i + 1)
                    if s == 3 and last_pair(i):
                        dve.wait_ge(f_biased, i + 2)
                    uses = 4 if s % 2 == 0 else 3
                    if s >= 2 or not first(i):
                        dve.wait_ge(stored[s % 2], 16 * (i * uses + s // 2))
                    nc.vector.tensor_tensor(oslice[:, s % 2, :], ring_c[k % RING_C][0:ROWS, :],
                                            fbuf[:, s * SW * C:(s + 1) * SW * C], ALU.add).then_inc(c_dve, 1)

                def ev_turn(i, ks):
                    for k in ks:
                        dve.wait_ge(pe_b, i * B_CHUNKS + tr_at(k) + 1)
                        turn_copy(nc.vector.tensor_copy, 1, k).then_inc(b_dve, 1)

                def ev_inv_h(i, k):
                    if k == 0:
                        dve.wait_ge(r_ready, i + 1)
                    if k % 4 == 0 and not first(i):
                        dve.wait_ge(c_dve, (i - 1) * C_DVE + (out_done(3) if k == 0 else C_DVE))
                    at = fin_at(k)
                    dve.wait_ge(pe_b, i * B_CHUNKS + at + 1)
                    nc.vector.tensor_tensor(fbuf[:, k * 7 * C:(k + 1) * 7 * C], ring_b[at % RING_B][0:ROWS, 0:7 * C],
                                            r_nat[:, k * 7 * C:(k + 1) * 7 * C], ALU.add).then_inc(b_dve, 1)

                def ln2_stats(i, k):
                    dve.wait_ge(b_dve, i * B_DVE + b_done("dve", fin_at(k)))
                    last = stat_w(fbuf, range(7 * k, 7 * k + 7))
                    if k == 7 or k == 3 and last_pair(i):
                        last.then_inc(ln_step[1], 1)

                def step(i, ahead, behind):
                    def slice_(s, before, after):
                        before()
                        if behind and s < SLICES - 1:
                            ev_rest(i - 1, s + 1)
                        after()
                        if behind:
                            ev_mlp(i - 1, s)

                    def next_(what, *args):
                        if ahead:
                            what(i + 1, *args)

                    if behind:
                        for k in range(1, 8):
                            ln2_stats(i - 1, k)
                        ln2(i - 1)
                    next_(ev_whiten, [0, 1])
                    ev_layer_1(i)
                    if behind:
                        ev_rest(i - 1, 0)
                    slice_(0, lambda: next_(ev_whiten, [2, 3, 4, 5]), lambda: next_(ev_whiten, [6]))
                    slice_(1, lambda: (ev_layer_2(i, 0, [0, 1]), next_(ln1_stats, [0]), ev_layer_2(i, 0, [2])),
                           lambda: (ev_layer_2(i, 0, [3]), next_(ln1_stats, [1])))
                    slice_(2, lambda: (next_(ln1_stats, [2]), ev_layer_2(i, 1, [0]), next_(ln1_stats, [3]),
                                       ev_layer_2(i, 1, [1, 2])),
                           lambda: (ev_layer_2(i, 1, [3]), next_(ln1_stats, [4])))
                    slice_(3, lambda: (next_(ln1_stats, [5, 6, 7]), next_(mean_rstd, 0)), lambda: next_(ln1_subtract, 0))
                    slice_(4, lambda: (next_(ln1_rstd, 0), next_(ln1_last, 0)), lambda: next_(ln1_subtract, 1))
                    slice_(5, lambda: (next_(ln1_rstd, 1), ev_turn(i, [0, 1, 2])),
                           lambda: (ev_turn(i, [3]), next_(ln1_last, 1)))
                    def end_of_filter(ks):
                        for k in ks:
                            ev_turn(i, [4 + k])
                            ev_inv_h(i, k)
                            if not ahead and k > 0:
                                ln2_stats(i, k - 1)
                                if k == 3:
                                    ln2_stats(i, 3)

                    slice_(6, lambda: end_of_filter([0, 1, 2]), lambda: end_of_filter([3]))
                    if ahead:
                        ev_inv_h(i, 4)
                        ln2_stats(i, 0)
                        for k in range(5, 8):
                            ev_inv_h(i, k)

                def last_mlp(i):
                    mean_rstd(i, 1, 0)
                    subtract_mean(fbuf, n2, 1, 0)
                    multiply_rstd(n2, i, 1, 0).then_inc(n2_ready, 1)
                    ev_rest(i, 0)
                    for k in range(4, 8):
                        ev_inv_h(i, k)
                    ev_rest(i, 1)
                    ln2_stats(i, 4)
                    ln2_stats(i, 5)
                    ev_mlp(i, 0)
                    ln2_stats(i, 6)
                    ln2_stats(i, 7)
                    mean_rstd(i, 1, 1)
                    ev_rest(i, 2)
                    ev_mlp(i, 1)
                    subtract_mean(fbuf, n2, 1, 1)
                    multiply_rstd(n2, i, 1, 1).then_inc(n2_ready, 1)
                    ev_rest(i, 3)
                    ev_mlp(i, 2)
                    for s in range(3, SLICES):
                        if s < SLICES - 1:
                            ev_rest(i, s + 1)
                        ev_mlp(i, s)

                def first_h():
                    for k in range(7):
                        ev_whiten(0, [k])
                        dve.wait_ge(a_dve, k + 1)
                        last = stat_w(ybuf, range(8 * k, 8 * k + 8))
                    last.then_inc(ln_step[0], 1)
                    mean_rstd(0, 0)
                    for k in range(2):
                        ln1_subtract(0, k)
                        ln1_rstd(0, k)
                        if k == 0:
                            ln1_last(0, 0)
                    ln1_gain(0, 1).then_inc(h0_step, 1)
                    dve.wait_ge(h0_step, 1)
                    nc.vector.tensor_tensor(half_w(h_nat, 1), half_w(h_nat, 1), row("b1", WP), ALU.add).then_inc(h0_half, 1)

                covariance_and_factor()
                first_h()
                step(0, True, False)
                with dve.Fori(1, PAIRS - 1) as i:
                    step(i, True, True)
                step(PAIRS - 1, False, True)
                last_mlp(PAIRS - 1)

            @block.tensor
            def _(pe):
                def covariance():
                    pe.wait_ge(s_ones, 1)
                    pe.wait_ge(s_first[0], 16)
                    nc.tensor.matmul(pil, pilot_w[:], xin[:, 0:C], start=True, stop=True).then_inc(s_pilot, 1)

                    def gram_tile(j, count, first_tile):
                        for w in range(WP):
                            if first_tile and w % 7 == 0 and w < 21:
                                pe.wait_ge(s_cent_part, w // 7 + 1)
                            if w == (21 if first_tile else 0):
                                pe.wait_ge(s_cent, count)
                            last = nc.tensor.matmul(gram, cent[j][:, w * CW:w * CW + 2 * C], cent[j][:, w * CW:w * CW + CW],
                                                    start=(first_tile and w == 0), stop=False, skip_group_check=True)
                        last.then_inc(s_gram, 1)

                    gram_tile(0, 1, True)
                    gram_tile(1, 2, False)
                    with pe.Fori(1, PAIRS // 2) as i:
                        for j in range(2):
                            gram_tile(j, 2 * i + 1 + j, False)
                    pe.wait_ge(s_cst, 16)
                    pe.wait_ge(s_dve, DV_WEIGHTS + 3)
                    nc.tensor.matmul(row_ps, gtmp[:, C:C + 1], ident[0:C, 0:C], start=True, stop=True).then_inc(s_pe, 1)
                    pe.wait_ge(s_dve, DV_WEIGHTS + 4)
                    nc.tensor.matmul(outer_ps, rowd[:, 0:C], rowd[:, 0:C], start=True, stop=True).then_inc(s_pe, 1)
                    pe.wait_ge(s_dve, DV_WEIGHTS + 6)
                    nc.tensor.matmul(mcol_ps, rowd[:, 2 * C:4 * C], ident[0:1, 0:1], start=True, stop=True).then_inc(s_pe, 1)
                    pe.wait_ge(s_prm, 16)
                    pe.wait_ge(s_dve, DV_MEAN)
                    for m in range(2):
                        last = nc.tensor.matmul(hb_ps[:, m:m + 1], pp("mw1", C)[:, HH * m:HH * m + HH], pp("b2", C),
                                                start=True, stop=True)
                    last.then_inc(s_pe, 1)

                def factor():
                    for k in range(C - 1):
                        j = max(k - 1, 0)
                        rows = elim[:, j % 2, k:k + C + 1]
                        pe.wait_ge(s_dve, DV_COV + 4 * j)
                        one = nc.tensor.matmul(rowk_ps[k % 2], ident[0:C, k:k + 1].broadcast_to((C, C)), rows,
                                               start=True, stop=(k == 0))
                        if k > 0:
                            pe.wait_ge(s_dve, DV_COV + 4 * j + 2)
                            one = nc.tensor.matmul(rowk_ps[k % 2], ahead_v[:, j % 2:j % 2 + 1].broadcast_to((C, C)),
                                                   rows, start=False, stop=True)
                        one.then_inc(s_pe, 1)
                        if k % 2 == 0 and 8 <= k < 8 + 2 * 7:
                            transpose_x(0, [(k - 8) // 2])
                    pe.wait_ge(s_dve, DV_W)
                    nc.tensor.transpose(wt_ps, ediag[:], ident[0:C, 0:C]).then_inc(s_pe, 1)

                def free_b(i, k):
                    j = k - RING_B
                    if j < 0:
                        if first(i):
                            return ring_b[k % RING_B]
                        i, j = i - 1, j + B_CHUNKS
                    if "act" in B_READERS[j]:
                        pe.wait_ge(b_act, i * B_ACT + b_done("act", j))
                    if "dve" in B_READERS[j]:
                        pe.wait_ge(b_dve, i * B_DVE + b_done("dve", j))
                    return ring_b[k % RING_B]

                def free_c(i, k):
                    j = k - RING_C
                    if j < 0:
                        if first(i):
                            return ring_c[k % RING_C]
                        who, n = c_reader(j + C_CHUNKS)
                        i = i - 1
                    else:
                        who, n = c_reader(j)
                    if who == "act":
                        pe.wait_ge(c_act, i * C_ACT + n)
                    else:
                        pe.wait_ge(c_dve, i * C_DVE + n)
                    return ring_c[k % RING_C]

                def transpose_x(i, ks):
                    if 0 in ks:
                        pe.wait_ge(x_in, 16 * i + 16)
                    for k in ks:
                        if k >= RING_A:
                            pe.wait_ge(a_act, i * 7 + k - RING_A + 1)
                        elif not first(i):
                            pe.wait_ge(a_dve, i * 7 - RING_A + k + 1)
                        t = ring_a[k % RING_A]
                        for j in range(4):
                            w = 4 * k + j
                            last = nc.tensor.transpose(t[:, j * ROWS:(j + 1) * ROWS], xin[:, w * 128:w * 128 + 128],
                                                       ident[0:ROWS, 0:ROWS])
                        last.then_inc(pe_a, 1)

                def whiten(i, ks):
                    pe.wait_ge(a_act, i * 7 + 7)
                    for k in ks:
                        if k + 7 - RING_A >= 7:
                            pe.wait_ge(a_dve, i * 7 + k - RING_A + 1)
                        t = ring_a[(k + 7) % RING_A]
                        for j in range(4):
                            w = 4 * k + j
                            last = nc.tensor.matmul(t[0:ROWS, j * 128:(j + 1) * 128], xT[:, w * ROWS:(w + 1) * ROWS],
                                                    wy[:], start=True, stop=True)
                        last.then_inc(pe_a, 1)

                def dft_h(i):
                    pe.wait_ge(h_ready, i * 2 + 1)
                    if first(i):
                        pe.wait_ge(h0_half, 1)
                    for k in range(8):
                        t = free_b(i, S1 + k)
                        for j in range(4):
                            last = nc.tensor.matmul(t[0:ROWS, j * 2 * KR:(j + 1) * 2 * KR], h_w[:, :, 4 * k + j],
                                                    cc("f1", ROWS), start=True, stop=True)
                        last.then_inc(pe_b, 1)

                def dft_w(i):
                    pe.wait_ge(b_act, i * B_ACT + b_done("act", S2 - 1))
                    for k in range(8):
                        t = free_b(i, S2 + k)
                        for j in range(min(4, KF - 4 * k)):
                            last = nc.tensor.matmul(t[:, j * 4 * KF:(j + 1) * 4 * KF], u_r[0:ROWS, (4 * k + j) * 128:(4 * k + j + 1) * 128],
                                                    cc("f2", ROWS), start=True, stop=True)
                        last.then_inc(pe_b, 1)

                def layer_1(i):
                    for k in range(8):
                        part, half, b = k // 4, k // 2 % 2, k % 2
                        pe.wait_ge(b_act, i * B_ACT + b_done("act", S2 + 3 if part == 0 else L1 - 1))
                        t = free_b(i, L1 + k)
                        a, z = L1_PARTS[part]
                        nc.tensor.matmul(t[:, 0:(z - a) * KF], w1s[:, 128 * half:128 * half + 128],
                                         p_v[:, b, half, a:z, :].rearrange("p k w -> p (k w)"),
                                         start=True, stop=True).then_inc(pe_b, 1)

                def layer_2(i, half, k):
                    if half == 0 and k == 0:
                        pe.wait_ge(b_act, i * B_ACT + b_done("act", L2 - 1))
                        pe.wait_ge(b_dve, i * B_DVE + b_done("dve", L2 - 1))
                    t = free_b(i, L2 + 4 * half + k)
                    for j in range(L2_KP[k]):
                        kh = 2 * (4 * k + j)
                        last = nc.tensor.matmul(t[0:2 * KR, j * 128:j * 128 + 128],
                                                o_g[:, (half * KF + kh) * KR:(half * KF + kh + 2) * KR],
                                                w2s[:, 128 * half:128 * half + 128], start=True, stop=True)
                    last.then_inc(pe_b, 1)

                def inverse(r, n):
                    table = cc("invw", n * KR)[:, 224 * r:224 * r + 224]
                    return table if n == 2 else table.rearrange("p (w m) -> p w m", m=4)[:, :, 0:2]

                def inv_w(i, ks):
                    for k in ks:
                        pe.wait_ge(y_ready, i * 8 + 4 + k // 2 + 1)
                        t = free_b(i, INVW + k)
                        for j in range(min(2, KHP - 2 * k)):
                            kp = 2 * k + j
                            n = min(2, KF - 2 * kp)
                            for r in range(2):
                                last = nc.tensor.matmul(t[:, j * 224:j * 224 + n * 112],
                                                        y_v[0:n * KR, kp, 128 * r:128 * r + 128],
                                                        inverse(r, n), start=(r == 0), stop=(r == 1))
                        last.then_inc(pe_b, 1)

                def turn(i, ks):
                    pe.wait_ge(b_act, i * B_ACT + b_done("act", TR - 1))
                    for k in ks:
                        t = free_b(i, tr_at(k))
                        w0, n = TURN_WP[k]
                        for j in range(n):
                            last = nc.tensor.transpose(t[:, j * 128:j * 128 + 128],
                                                       u_r[:, (w0 + j) * 128:(w0 + j + 1) * 128], ident)
                        last.then_inc(pe_b, 1)

                def inv_h(i, k):
                    pe.wait_ge(b_act, i * B_ACT + b_done("act", tr_at(k)))
                    pe.wait_ge(b_dve, i * B_DVE + b_done("dve", tr_at(k)))
                    t = free_b(i, fin_at(k))
                    nc.tensor.matmul(t[0:ROWS, 0:7 * C], cc("invh", GR), o_g[0:GR, k * 7 * C:(k + 1) * 7 * C],
                                     start=True, stop=True).then_inc(pe_b, 1)

                def transpose_n(i, s):
                    k = 0 if s == 0 else 5 + 6 * (s - 1)
                    if s == 0:
                        pe.wait_ge(n2_ready, 2 * i + 1)
                    if s == 3:
                        pe.wait_ge(n2_ready, 2 * i + 2)
                    t = free_c(i, k)
                    for j in range(4):
                        w = 4 * s + j
                        last = nc.tensor.transpose(t[:, j * ROWS:(j + 1) * ROWS], n2[:, w * 128:w * 128 + 128],
                                                   ident[0:ROWS, 0:ROWS])
                    last.then_inc(pe_c, 1)

                def mlp(i, s, fill):
                    pe.wait_ge(c_dve, i * C_DVE + lo_done(s))
                    for v in range(2):
                        for m in range(2):
                            if m == 1:
                                fill(v)
                            t = free_c(i, 1 + 6 * s + 2 * v + m)
                            for wt, p in ((mw1h, 0), (mw1l, 1)):
                                last = nc.tensor.matmul(t[:, 0:4 * ROWS], wt[:, HH * m:HH * m + HH], n2T[:, v, :],
                                                        start=(p == 0), stop=(p == 1))
                            last.then_inc(pe_c, 1)
                    fill(2)
                    if s < SLICES - 1:
                        transpose_n(i, s + 1)
                    fill(3)
                    k = 6 + 6 * s if s < SLICES - 1 else C_CHUNKS - 1
                    t = free_c(i, k)
                    pe.wait_ge(c_act, i * C_ACT + 4 * s + 4)
                    for w in range(SW):
                        at, zeros = (w * C, 32) if w < SW - 1 else (w * C - 32, 0)
                        for m in range(2):
                            last = nc.tensor.matmul(t[0:ROWS, at:at + 96],
                                                    hid[:, m, w % 2, (w // 2) * ROWS:(w // 2 + 1) * ROWS],
                                                    pp("mw2")[:, 128 * m + zeros:128 * m + zeros + 96],
                                                    start=(w == 0 and m == 0), stop=(w == SW - 1 and m == 1),
                                                    skip_group_check=True)
                    last.then_inc(pe_c, 1)

                def step(i, ahead, ahead2, behind):
                    def slice_(s, fill):
                        if behind:
                            mlp(i - 1, s, fill)
                        else:
                            for j in range(4):
                                fill(j)

                    def whiten_next(j):
                        if ahead and j < 3:
                            whiten(i + 1, [4 + j])

                    def and_x(s, what):
                        def both(j):
                            what(j)
                            if ahead2:
                                transpose_x(i + 2, X_BESIDE[s][j])
                        return both

                    dft_h(i)
                    if ahead:
                        whiten(i + 1, [0])
                    dft_w(i)
                    if ahead:
                        whiten(i + 1, [1])
                    layer_1(i)
                    if behind:
                        transpose_n(i - 1, 0)
                    if ahead:
                        whiten(i + 1, [2, 3])
                    slice_(0, whiten_next)
                    slice_(1, and_x(1, lambda j: layer_2(i, 0, j)))
                    slice_(2, and_x(2, lambda j: layer_2(i, 1, j)))
                    slice_(3, and_x(3, lambda j: inv_w(i, [j])))
                    slice_(4, lambda j: inv_w(i, [4 + j]))
                    slice_(5, lambda j: turn(i, [j]))
                    slice_(6, lambda j: (turn(i, [4 + j]), inv_h(i, j)))
                    for k in range(4, 8):
                        inv_h(i, k)

                covariance()
                factor()
                pe.wait_ge(s_dve, DV_WY)
                pe.wait_ge(s_ones, MEMSETS)
                whiten(0, range(7))
                transpose_x(1, range(7))
                step(0, True, True, False)
                with pe.Fori(1, PAIRS - 2) as i:
                    step(i, True, True, True)
                step(PAIRS - 2, True, False, True)
                step(PAIRS - 1, False, False, True)
                transpose_n(PAIRS - 1, 0)
                for s in range(SLICES):
                    mlp(PAIRS - 1, s, lambda j: None)

            @block.scalar
            def _(act):
                def ev_x(i, ks):
                    for k in ks:
                        act.wait_ge(pe_a, i * A_CHUNKS + k + 1)
                        nc.scalar.activation(xT[:, k * 4 * ROWS:(k + 1) * 4 * ROWS], ring_a[k % RING_A][:, 0:4 * ROWS],
                                             ACT.Identity, bias=negm[:]).then_inc(a_act, 1)

                def ev_dft_h(i):
                    for k in range(8):
                        act.wait_ge(pe_b, i * B_CHUNKS + S1 + k + 1)
                        nc.scalar.copy(u_v[:, :, 4 * k:4 * k + 4],
                                       ring_b[k % RING_B][0:ROWS, 0:8 * KR].rearrange("p (j m) -> p m j", j=4)
                                       ).then_inc(b_act, 1)

                def ev_dft_w(i):
                    for k in range(8):
                        act.wait_ge(pe_b, i * B_CHUNKS + S2 + k + 1)
                        n = min(4, KF - 4 * k)
                        t = ring_b[k % RING_B][:, 0:n * 4 * KF].rearrange("p (k s h w) -> p s h k w", s=2, h=2, w=KF)
                        for b in range(2):
                            for s in range(2):
                                last = nc.scalar.copy(p_v[C * s:C * s + C, b, :, 4 * k:4 * k + n, :],
                                                      t[C * b:C * b + C, s])
                        last.then_inc(b_act, 1)

                def ev_layer_1(i):
                    for k in range(8):
                        if k not in L1_DVE:
                            act.wait_ge(pe_b, i * B_CHUNKS + L1 + k + 1)
                            for dst, src, bias in layer_1_parts(k):
                                last = nc.scalar.activation(dst, src, ACT.Relu, bias=bias)
                            last.then_inc(b_act, 1)

                def ev_inv_w(i, ks):
                    for k in ks:
                        act.wait_ge(pe_b, i * B_CHUNKS + INVW + k + 1)
                        if k < 7:
                            src = ring_b[k % RING_B][:, 0:448].rearrange("p (j w m) -> p w j m", j=2, m=4)
                            dst = r_v[:, :, 8 * k:8 * k + 8].rearrange("p w (j m) -> p w j m", m=4)
                        else:
                            src = ring_b[k % RING_B][:, 0:112].rearrange("p (w m) -> p w m", m=2)
                            dst = r_v[:, :, 8 * k:8 * k + 2]
                        nc.scalar.copy(dst, src).then_inc(b_act, 1)

                def ev_turn(i, ks):
                    for k in ks:
                        act.wait_ge(pe_b, i * B_CHUNKS + tr_at(k) + 1)
                        turn_copy(nc.scalar.copy, 0, k).then_inc(b_act, 1)

                def ev_n2(i, s):
                    k = 0 if s == 0 else 5 + 6 * (s - 1)
                    act.wait_ge(pe_c, i * C_CHUNKS + k + 1)
                    for v in range(2):
                        nc.scalar.copy(n2T[C * v:C * v + C, v, :],
                                       ring_c[k % RING_C][C * v:C * v + C, 0:4 * ROWS]).then_inc(hi_ready, 1)

                def gelu(i, s, fill):
                    for q in range(4):
                        k = 1 + 6 * s + q
                        act.wait_ge(pe_c, i * C_CHUNKS + k + 1)
                        nc.scalar.activation(hid[:, q % 2, q // 2, :], ring_c[k % RING_C][:, 0:4 * ROWS], ACT.Gelu,
                                             bias=hbias[:, q % 2:q % 2 + 1]).then_inc(c_act, 1)
                        if q % 2 == 0:
                            fill(q // 2)
                    fill(2)
                    if s < SLICES - 1:
                        ev_n2(i, s + 1)
                    fill(3)

                def shrink(i, c):
                    n = L2_KP[c % 4] * 128
                    v = layer2[:, c % L2_BUFS, 0:n]
                    act.wait_ge(b_dve, i * B_DVE + b_done("dve", L2 + c))
                    if c >= L2_BUFS or not first(i):
                        act.wait_ge(y_ready, i * 8 + c - L2_BUFS + 1)
                    nc.scalar.activation(over[:, c % L2_BUFS, 0:n], v, ACT.Relu, bias=neg_lam[0:2 * KR, :])
                    nc.scalar.activation(under[:, c % L2_BUFS, 0:n], v, ACT.Relu, bias=neg_lam[0:2 * KR, :],
                                         scale=-1.0).then_inc(shrunk, 1)

                def step(i, ahead2, behind):
                    def slice_(s, fill):
                        if behind:
                            gelu(i - 1, s, fill)
                        else:
                            for j in range(4):
                                fill(j)

                    def x_next(s, j):
                        if ahead2:
                            ev_x(i + 2, X_BESIDE[s][j])

                    def shrink_late(s, j):
                        x_next(s, j)
                        c = 4 * (s - 1) + j - 1
                        if c >= 0:
                            shrink(i, c)

                    def first_inv_w(j):
                        if j == 0:
                            shrink(i, 7)
                        ev_inv_w(i, [j])
                        x_next(3, j)

                    ev_dft_h(i)
                    ev_dft_w(i)
                    ev_layer_1(i)
                    if behind:
                        ev_n2(i - 1, 0)
                    slice_(0, lambda j: None)
                    slice_(1, lambda j: shrink_late(1, j))
                    slice_(2, lambda j: shrink_late(2, j))
                    slice_(3, first_inv_w)
                    slice_(4, lambda j: ev_inv_w(i, [4 + j]))
                    slice_(5, lambda j: ev_turn(i, [j]))
                    slice_(6, lambda j: ev_turn(i, [4 + j]))

                act.wait_ge(s_dve, DV_MEAN)
                act.wait_ge(s_ones, MEMSETS)
                act.wait_ge(s_prm, 16)
                ev_x(0, range(7))
                ev_x(1, range(7))
                step(0, True, False)
                act.wait_ge(s_dve, DV_ALL)
                with act.Fori(1, PAIRS - 2) as i:
                    step(i, True, True)
                step(PAIRS - 2, False, True)
                step(PAIRS - 1, False, True)
                ev_n2(PAIRS - 1, 0)
                for s in range(SLICES):
                    gelu(PAIRS - 1, s, lambda j: None)


def constants():
    at, n = offsets(CONST_COLS)
    c = np.zeros((128, n), np.float32)

    def put(name, m):
        c[:m.shape[0], at[name][0]:at[name][1]] = m.reshape(m.shape[0], -1)

    pos, k = np.arange(H), np.arange(KF)
    cos = np.cos(2 * np.pi * (np.outer(pos, k) % H) / H)
    sin = np.sin(2 * np.pi * (np.outer(pos, k) % H) / H)
    f1 = np.zeros((2, H, KF, 2, 2))
    for b in range(2):
        f1[b, :, :, b, 0] = cos / H
        f1[b, :, :, b, 1] = -sin / H
    put("f1", f1.reshape(ROWS, -1))
    f2 = np.zeros((W, 2, 2, 2, KF))
    for h in range(2):
        f2[:, h, 0, h, :] = cos
        f2[:, h, 1, h, :] = sin
    put("f2", f2.reshape(ROWS, -1))
    wk = np.where((k == 0) | (k == KF - 1), 0.5, 1.0)
    inv = np.zeros((2, 2, KF, 2, W, 2, 2))
    for q in range(2):
        for s, sign in enumerate((1.0, -1.0)):
            inv[q, s, :, 0, :, q, 0] = (wk * cos).T
            inv[q, s, :, 0, :, q, 1] = sign * (wk * sin).T
            inv[q, s, :, 1, :, q, 0] = -(wk * sin).T
            inv[q, s, :, 1, :, q, 1] = sign * (wk * cos).T
    put("invw", inv.reshape(2 * KR, -1))
    ih = np.zeros((2, 64, 2, H))
    for b in range(2):
        ih[b, 0:KR:2, b] = (2 * wk * cos).T / H
        ih[b, 1:KR:2, b] = -(2 * wk * sin).T / H
    put("invh", ih.reshape(128, -1))
    same = np.kron(np.eye(CH // BS), np.ones((BS, BS)))
    m1 = np.zeros((2, 2, CH, 2, 2, CH))
    for cs, r in ((0, 0), (0, 1), (1, 0), (1, 1)):
        for s, sign in enumerate((1.0, -1.0)):
            to_re = (cs == r)
            coef = {(0, 0): 1.0, (1, 1): sign, (0, 1): sign, (1, 0): -1.0}[cs, r]
            m1[cs, r, :, s, 0] = same * coef * (1.0 if to_re else -1.0)
            m1[cs, r, :, s, 1] = same * coef
    put("mask1", m1.reshape(128, -1))
    m2 = np.zeros((2, 2, CH, 2, 2, CH))
    for b in range(2):
        for r in range(2):
            m2[b, r, :, 0, b] = same * (1.0 if r == 0 else -1.0)
            m2[b, r, :, 1, b] = same
    put("mask2", m2.reshape(128, -1))
    put("below", -np.tril(np.ones((C, C)), -1))
    put("minus", -np.eye(C))
    put("ident", np.eye(128))
    return c


def layout(i):
    at, n = offsets(PARAM_COLS)
    p = np.zeros((128, n), np.float32)

    def put(name, m):
        p[:m.shape[0], at[name][0]:at[name][1]] = m.reshape(m.shape[0], -1)

    def rows(v):
        return np.broadcast_to(v.reshape(1, -1), (128, v.size))

    G = CH // BS
    w1 = i["L1_conv_w1"].reshape(2, 2, G, BS, BS)
    w2 = i["L1_conv_w2"].reshape(2, 2, G, BS, BS)
    a = np.zeros((2, 2, G, BS, 2, 2, 2, G, BS), np.float32)
    for cs in range(2):
        for r in range(2):
            for ro in range(2):
                part = ro if cs == r else 1 - ro
                a[cs, r, :, :, :, :, ro] = w1[part].transpose(1, 2, 0, 3)[:, :, :, None, None, :]
    put("w1", a.reshape(128, -1))
    a = np.zeros((2, 2, G, BS, 2, 2, 2, G, BS), np.float32)
    for r in range(2):
        for ro in range(2):
            part = ro if r == 0 else 1 - ro
            a[:, r, :, :, :, ro] = w2[part].transpose(1, 2, 0, 3)[None, :, :, :, None, None, :]
    put("w2", a.reshape(128, -1))
    put("mw1", np.tile(i["L1_conv_mw1"], (2, 1)))
    m = np.zeros((HH, 2, 128), np.float32)
    m[:, :, 32:32 + C] = i["L1_conv_mw2"].reshape(2, HH, C).transpose(1, 0, 2)
    put("mw2", m)
    put("beta", rows(i["L0_conv_beta"]))
    put("g1", rows(i["L1_conv_n1_g"]))
    put("b1", rows(i["L1_conv_n1_b"]))
    put("mb2", rows(i["L1_conv_mb2"]))
    fb2 = i["L1_conv_b2"].reshape(2, 2, CH).transpose(1, 0, 2)
    put("fb2", rows(np.broadcast_to(fb2[:, :, None, :], (2, 2, 2, CH))))
    put("gamma", i["L0_conv_gamma"].reshape(C, 1))
    put("g2", np.tile(i["L1_conv_n2_g"], 2).reshape(128, 1))
    put("b2", np.tile(i["L1_conv_n2_b"], 2).reshape(128, 1))
    fb1 = i["L1_conv_b1"].reshape(2, 2, CH).transpose(0, 2, 1)
    put("fb1", np.broadcast_to(fb1[None], (2, 2, CH, 2)).reshape(128, 2))
    put("mb1", i["L1_conv_mb1"].reshape(2, HH).T)
    return p


def kernel(**inputs):
    import numpy as _np
    import concourse.bacc as _bacc
    from concourse.bass_utils import run_bass_kernel_spmd as _run

    i = {k: _np.asarray(v) for k, v in inputs.items()}
    arrays = {"x_dram": _np.ascontiguousarray(i["x"]), "consts_dram": constants(), "params_dram": layout(i)}
    nc = _bacc.Bacc("TRN2", target_bir_lowering=False, num_devices=1)
    aps = {k: nc.dram_tensor(k, v.shape, F32, kind="ExternalInput").ap() for k, v in arrays.items()}
    out = nc.dram_tensor("out_dram", (B, H, W, C), F32, kind="ExternalOutput").ap()
    build(nc, aps["x_dram"], aps["consts_dram"], aps["params_dram"], out)
    r = _run(nc, [arrays], core_ids=[0])
    return r.results[0]["out_dram"]
```
